# Optimizing a Trainium2 kernel written in Bass

```python
import numpy as np
import jax
import jax.numpy as jnp

def _softmax(x, axis=-1):
    return jax.nn.softmax(x, axis=axis)

def _gelu(x):
    return jax.nn.gelu(x, approximate=True)

def _silu(x):
    return jax.nn.silu(x)

def _sigmoid(x):
    return jax.nn.sigmoid(x)

def _layernorm(x, axis=-1, eps=1e-05):
    m = jnp.mean(x, axis=axis, keepdims=True)
    v = jnp.var(x, axis=axis, keepdims=True)
    return (x - m) / jnp.sqrt(v + eps)

def _scatter_add(tgt, idx, src, axis=0):
    return tgt.at[idx].add(src)

def _segment_sum(src, seg, n):
    return jax.ops.segment_sum(src, seg, n)
kernel_name = 'mk_adaln_d1_jaxref_r8_268de6'

def setup_inputs(seed: int=0):
    np.random.seed(seed)
    _w = jnp.asarray

    def _L0_attn_setup():
        import jax, jax.numpy as jnp
        import numpy as np
        B, L, D = (4, 512, 128)
        DS, EXP, DC = (16, 2, 4)
        DI = EXP * D
        K_SYM = max(3, 2 * DC + 1)

        def _linear(x, w, b):
            return jnp.einsum('blc,oc->blo', x, w) + b

        def _dwconv(x, kernel, bias, pad_l, pad_r):
            y = jax.lax.conv_general_dilated(x.transpose(0, 2, 1), kernel, window_strides=(1,), padding=[(pad_l, pad_r)], dimension_numbers=('NCH', 'OIH', 'NCH'), feature_group_count=x.shape[-1])
            return y.transpose(0, 2, 1) + bias

        def _rmsnorm(x, w, eps=1e-06):
            scale = jax.lax.rsqrt(jnp.mean(x * x, axis=-1, keepdims=True) + eps)
            return w * x * scale
        key = jax.random.key(seed)
        ks = jax.random.split(key, 12)

        def n(k, shape, s=0.02):
            return jax.random.normal(k, shape, jnp.float32) * s
        return {'x': jax.random.normal(ks[0], (B, L, D), jnp.float32), 'norm_w': jnp.ones((D,), jnp.float32), 'in_w': n(ks[1], (2 * DI, D)), 'in_b': jnp.zeros((2 * DI,), jnp.float32), 'dwa_k': n(ks[2], (DI, 1, DC)), 'dwa_b': jnp.zeros((DI,), jnp.float32), 'A': n(ks[3], (DI, DS)), 'Bm': n(ks[4], (DS, DI)), 'sym_k': n(ks[5], (DI, 1, K_SYM)), 'sym_b': jnp.zeros((DI,), jnp.float32), 'pw_w': n(ks[6], (DI, DI)), 'pw_b': jnp.zeros((DI,), jnp.float32), 'ha_w': n(ks[7], (DI // 2, DI)), 'ha_b': jnp.zeros((DI // 2,), jnp.float32), 'hb_w': n(ks[8], (DI // 2, DI)), 'hb_b': jnp.zeros((DI // 2,), jnp.float32), 'fuse_w': n(ks[9], (DI, DI)), 'fuse_b': jnp.zeros((DI,), jnp.float32), 'out_w': n(ks[10], (D, DI)), 'out_b': jnp.zeros((D,), jnp.float32)}
    _L0_attn_in = _L0_attn_setup()

    def _L0_ffn_setup():
        import jax, jax.numpy as jnp
        import numpy as np
        NUM_EXPERTS = 160
        TOP_K = 8
        ROUTED_SCALE = 2.5
        HIDDEN = 128
        INTER = 64
        key = jax.random.key(seed)
        ks = jax.random.split(key, 7)
        B, S = (1, 256)
        return {'hidden_states': jax.random.normal(ks[0], (B, S, HIDDEN), dtype=jnp.float32), 'router_w': jax.random.normal(ks[1], (NUM_EXPERTS, HIDDEN), dtype=jnp.float32) * 0.02, 'expert_bias': jnp.zeros((NUM_EXPERTS,), dtype=jnp.float32), 'w_gate': jax.random.normal(ks[2], (NUM_EXPERTS, INTER, HIDDEN), dtype=jnp.float32) * 0.02, 'w_down': jax.random.normal(ks[3], (NUM_EXPERTS, HIDDEN, INTER), dtype=jnp.float32) * 0.02, 'w_gate_shared': jax.random.normal(ks[4], (INTER, HIDDEN), dtype=jnp.float32) * 0.02, 'w_down_shared': jax.random.normal(ks[5], (HIDDEN, INTER), dtype=jnp.float32) * 0.02}
    _L0_ffn_in = _L0_ffn_setup()
    _L0_c = _w((lambda *s: np.random.randn(*s).astype(np.float32) * 0.05)(4, 128))
    _L0_wmod = _w((lambda *s: np.random.randn(*s).astype(np.float32) * 0.05)(128, 6 * 128) * 128 ** (-0.5))
    _d = {'L0_attn_x': _L0_attn_in['x'], 'L0_attn_norm_w': _L0_attn_in['norm_w'], 'L0_attn_in_w': _L0_attn_in['in_w'], 'L0_attn_in_b': _L0_attn_in['in_b'], 'L0_attn_dwa_k': _L0_attn_in['dwa_k'], 'L0_attn_dwa_b': _L0_attn_in['dwa_b'], 'L0_attn_A': _L0_attn_in['A'], 'L0_attn_Bm': _L0_attn_in['Bm'], 'L0_attn_sym_k': _L0_attn_in['sym_k'], 'L0_attn_sym_b': _L0_attn_in['sym_b'], 'L0_attn_pw_w': _L0_attn_in['pw_w'], 'L0_attn_pw_b': _L0_attn_in['pw_b'], 'L0_attn_ha_w': _L0_attn_in['ha_w'], 'L0_attn_ha_b': _L0_attn_in['ha_b'], 'L0_attn_hb_w': _L0_attn_in['hb_w'], 'L0_attn_hb_b': _L0_attn_in['hb_b'], 'L0_attn_fuse_w': _L0_attn_in['fuse_w'], 'L0_attn_fuse_b': _L0_attn_in['fuse_b'], 'L0_attn_out_w': _L0_attn_in['out_w'], 'L0_attn_out_b': _L0_attn_in['out_b'], 'L0_ffn_router_w': _L0_ffn_in['router_w'], 'L0_ffn_expert_bias': _L0_ffn_in['expert_bias'], 'L0_ffn_w_gate': _L0_ffn_in['w_gate'], 'L0_ffn_w_down': _L0_ffn_in['w_down'], 'L0_ffn_w_gate_shared': _L0_ffn_in['w_gate_shared'], 'L0_ffn_w_down_shared': _L0_ffn_in['w_down_shared'], 'L0_c': _L0_c, 'L0_wmod': _L0_wmod}
    _x0 = _d['L0_attn_x']
    _d['L0_attn_x'] = jax.random.normal(jax.random.fold_in(jax.random.key(seed), 1), (4, 512, 128), dtype=_x0.dtype)
    del _x0
    return _d

def reference(L0_attn_x, L0_attn_norm_w, L0_attn_in_w, L0_attn_in_b, L0_attn_dwa_k, L0_attn_dwa_b, L0_attn_A, L0_attn_Bm, L0_attn_sym_k, L0_attn_sym_b, L0_attn_pw_w, L0_attn_pw_b, L0_attn_ha_w, L0_attn_ha_b, L0_attn_hb_w, L0_attn_hb_b, L0_attn_fuse_w, L0_attn_fuse_b, L0_attn_out_w, L0_attn_out_b, L0_ffn_router_w, L0_ffn_expert_bias, L0_ffn_w_gate, L0_ffn_w_down, L0_ffn_w_gate_shared, L0_ffn_w_down_shared, L0_c, L0_wmod):

    def _L0_attn_ref(x, norm_w, in_w, in_b, dwa_k, dwa_b, A, Bm, sym_k, sym_b, pw_w, pw_b, ha_w, ha_b, hb_w, hb_b, fuse_w, fuse_b, out_w, out_b):
        import jax, jax.numpy as jnp
        import numpy as np
        B, L, D = (4, 512, 128)
        DS, EXP, DC = (16, 2, 4)
        DI = EXP * D
        K_SYM = max(3, 2 * DC + 1)

        def _linear(x, w, b):
            return jnp.einsum('blc,oc->blo', x, w) + b

        def _dwconv(x, kernel, bias, pad_l, pad_r):
            y = jax.lax.conv_general_dilated(x.transpose(0, 2, 1), kernel, window_strides=(1,), padding=[(pad_l, pad_r)], dimension_numbers=('NCH', 'OIH', 'NCH'), feature_group_count=x.shape[-1])
            return y.transpose(0, 2, 1) + bias

        def _rmsnorm(x, w, eps=1e-06):
            scale = jax.lax.rsqrt(jnp.mean(x * x, axis=-1, keepdims=True) + eps)
            return w * x * scale
        residual = x
        h = _rmsnorm(x, norm_w)
        h = _linear(h, in_w, in_b)
        gate, val = (h[..., :DI], h[..., DI:])
        gate = jax.nn.sigmoid(gate)
        a = _dwconv(val, dwa_k, dwa_b, 1, 2)
        a = jnp.einsum('bld,ds->bls', a, A)
        a = jnp.einsum('bls,sd->bld', a, Bm)
        b = _dwconv(val, sym_k, sym_b, K_SYM // 2, K_SYM // 2)
        b = jax.nn.silu(b)
        b = _linear(b, pw_w, pw_b)
        a = _linear(a, ha_w, ha_b)
        b = _linear(b, hb_w, hb_b)
        y = jnp.concatenate([a, b], axis=-1)
        y = _linear(y, fuse_w, fuse_b)
        y = gate * y
        y = _linear(y, out_w, out_b)
        return residual + y

    def _L0_ffn_ref(hidden_states, router_w, expert_bias, w_gate, w_down, w_gate_shared, w_down_shared):
        import jax, jax.numpy as jnp
        import numpy as np
        NUM_EXPERTS = 160
        TOP_K = 8
        ROUTED_SCALE = 2.5
        HIDDEN = 128
        INTER = 64
        B, S, H = hidden_states.shape
        x = hidden_states.reshape(-1, H)
        T = x.shape[0]
        logits = x @ router_w.T + expert_bias[None, :]
        probs = jax.nn.sigmoid(logits)
        top_w, top_idx = jax.lax.top_k(probs, TOP_K)
        top_w = top_w / (jnp.sum(top_w, axis=-1, keepdims=True) + 1e-09)
        top_w = top_w * ROUTED_SCALE
        combine = jnp.zeros((T, NUM_EXPERTS), dtype=x.dtype)
        combine = combine.at[jnp.arange(T)[:, None], top_idx].set(top_w)
        h1 = jax.nn.silu(jnp.einsum('th,eih->eti', x, w_gate))
        h1w = h1 * combine.T[:, :, None]
        routed = jnp.einsum('eti,ehi->th', h1w, w_down)
        shared = jax.nn.silu(x @ w_gate_shared.T) @ w_down_shared.T
        return (routed + shared).reshape(B, S, H)
    x = L0_attn_x
    mod = (_silu(L0_c) @ L0_wmod).reshape(L0_c.shape[0], 6, 1, -1)
    sa, ca, ga, sb, cb, gb = (mod[:, 0], mod[:, 1], mod[:, 2], mod[:, 3], mod[:, 4], mod[:, 5])
    ga = (2 * (ga >= 0) - 1) * jnp.maximum(jnp.abs(ga), 0.25)
    gb = (2 * (gb >= 0) - 1) * jnp.maximum(jnp.abs(gb), 0.25)
    h = _layernorm(x, axis=-1) * (1 + ca) + sa
    x = x + ga * _L0_attn_ref(h, L0_attn_norm_w, L0_attn_in_w, L0_attn_in_b, L0_attn_dwa_k, L0_attn_dwa_b, L0_attn_A, L0_attn_Bm, L0_attn_sym_k, L0_attn_sym_b, L0_attn_pw_w, L0_attn_pw_b, L0_attn_ha_w, L0_attn_ha_b, L0_attn_hb_w, L0_attn_hb_b, L0_attn_fuse_w, L0_attn_fuse_b, L0_attn_out_w, L0_attn_out_b)
    h = _layernorm(x, axis=-1) * (1 + cb) + sb
    x = x + gb * _L0_ffn_ref(h, L0_ffn_router_w, L0_ffn_expert_bias, L0_ffn_w_gate, L0_ffn_w_down, L0_ffn_w_gate_shared, L0_ffn_w_down_shared)
    return x

_drawn_inputs = setup_inputs


def setup_inputs(seed=0):
    import zlib

    import numpy as np

    out = dict(_drawn_inputs(seed))
    spreads = {'L0_attn_norm_w': (1.0, 0.6),
     'L0_attn_in_b': (0.0, 0.8),
     'L0_attn_dwa_b': (0.0, 0.8),
     'L0_attn_sym_b': (0.0, 0.8),
     'L0_attn_pw_b': (0.0, 0.8),
     'L0_attn_ha_b': (0.0, 0.8),
     'L0_attn_hb_b': (0.0, 0.8),
     'L0_attn_fuse_b': (0.0, 0.8),
     'L0_attn_out_b': (0.0, 1.67),
     'L0_ffn_expert_bias': (0.0, 0.8)}
    factors = {'L0_attn_in_w': 8.0,
     'L0_attn_dwa_k': 8.0,
     'L0_attn_A': 8.0,
     'L0_attn_Bm': 8.0,
     'L0_attn_sym_k': 8.0,
     'L0_attn_pw_w': 8.0,
     'L0_attn_ha_w': 8.0,
     'L0_attn_hb_w': 8.0,
     'L0_attn_fuse_w': 8.0,
     'L0_attn_out_w': 8.0,
     'L0_ffn_router_w': 8.0,
     'L0_ffn_w_gate': 8.0,
     'L0_ffn_w_down': 8.0,
     'L0_ffn_w_gate_shared': 8.0,
     'L0_ffn_w_down_shared': 8.0}
    for name, (base, spread) in spreads.items():
        noise = np.random.default_rng([zlib.crc32(name.encode()), seed]).standard_normal(out[name].shape)
        drawn = base * np.exp(spread * noise) if base else spread * noise
        out[name] = jnp.asarray(drawn.astype(out[name].dtype))
    for name, factor in factors.items():
        out[name] = (out[name] * factor).astype(out[name].dtype)
    return out
```

```python
from contextlib import ExitStack

import concourse.bass as bass
from concourse import mybir

F32 = mybir.dt.float32
F16 = mybir.dt.float16
BF16 = mybir.dt.bfloat16
ALU = mybir.AluOpType
ACT = mybir.ActivationFunctionType
AX = mybir.AxisListType

P = 128
B, L, D = 4, 512, 128
DI = 2 * D
ML = DI // P
DS, DC = 16, 4
KS = 2 * DC + 1
PADL = KS // 2
NT = L // P
E, TOPK, INTER = 160, 8, 64
ROUTED_SCALE = 2.5
STACKS, PARTS = 4, 3
ES = E // STACKS
GROUPS = ES // 2
BLOCKS = E // 2
LAG = 3
RING = 4
WS = 16.0
ES_SCALE = 64.0
PIECE = 8
NPIECE = BLOCKS // PIECE

V = {}
_at = 0
for _n, _w in (("norm_w", 1), ("in_b", 4), ("dwa_b", ML), ("sym_b", ML), ("pw_b", ML), ("fuse_b", ML),
               ("ha_b", 1), ("hb_b", 1), ("dwa_k", ML * DC), ("sym_k", ML * KS), ("A", ML * DS), ("BmT", ML * DS),
               ("cT", B)):
    V[_n] = (_at, _w)
    _at += _w
NV = _at
M = {}
_at = 0
for _n, _w in (("wmod", 6 * D), ("in_wT", 2 * DI), ("inv", ML * D), ("haT", ML * P), ("hbT", ML * P),
               ("pw", ML * DI), ("fuseT", ML * DI), ("outT", ML * D), ("rT", E), ("sgT", INTER)):
    M[_n] = (_at, _w)
    _at += _w
NM = _at


def build(nc, x, vecs, mats, sdT, rows, sel_c, idb_c, idf_c, wg, wd, out):
    with ExitStack() as ctx:
        def sb(name, shape, dt=F32):
            return ctx.enter_context(nc.sbuf_tensor(name, shape, dt))

        def sem(name):
            return ctx.enter_context(nc.semaphore(name))

        bank = [ctx.enter_context(nc.psum_tensor(f"bank{i}", [P, 512], F32)) for i in range(8)]
        up_ps, cb_ps, acc_ps = bank[0:2], bank[2:4], bank[4]
        pa, pb, pc = bank[5], bank[6], bank[7]

        vec = sb("vec", [P, NV])
        mat = sb("mat", [P, NM])
        idf = sb("idf", [P, P])
        room = [0]

        def over_mat(shape, dt=F32):
            words = shape[0] * shape[1] * (2 if dt == F16 else 4) // 4
            ap = mat[:, room[0]:room[0] + words]
            room[0] += words
            assert room[0] <= NM
            ap = ap if dt == F32 else ap.bitcast(dt)
            return ap.rearrange("p (a b) -> p a b", a=shape[0])

        sdf = sb("sdf", [INTER, P])
        brow = sb("brow", [P, E + D])
        sel = sb("sel", [P, GROUPS * P], BF16)
        idb = sb("idb", [P, P], BF16)

        def v(name, i=0, n=1):
            at = V[name][0] + i
            return vec[:, at:at + n]

        def m(name, i=0, n=None):
            at, w = M[name]
            return mat[:, at + i:at + (w if n is None else i + n)]

        ebias, outb = brow[:, 0:E], brow[:, E:E + D]

        win_h, win_l = sb("win_h", [P, 2 * DI], F16), sb("win_l", [P, 2 * DI], F16)
        wz_h, wz_l = sb("wz_h", [P, P], F16), sb("wz_l", [P, P], F16)
        wa_h, wa_l = sb("wa_h", [P, DI], F16), sb("wa_l", [P, DI], F16)
        wb_h, wb_l = sb("wb_h", [P, ML, DI], F16), sb("wb_l", [P, ML, DI], F16)
        wo_h, wo_l = sb("wo_h", [P, ML, D], F16), sb("wo_l", [P, ML, D], F16)
        wr_h, wr_l = sb("wr_h", [P, E], F16), sb("wr_l", [P, E], F16)
        sg_h, sg_l = sb("sg_h", [P, INTER], F16), sb("sg_l", [P, INTER], F16)
        sd_h, sd_l = sb("sd_h", [INTER, P], F16), sb("sd_l", [INTER, P], F16)
        ak = sb("ak", [P, ML, P])
        a1 = sb("a1", [P, ML, P])
        bm4 = sb("bm4", [P, ML, P])
        jb, bz, by = sb("jb", [P, 1]), sb("bz", [P, 1]), sb("by", [P, ML])
        sct = sb("sct", [P, B])
        mod = sb("mod", [P, B, 6 * D])

        wg_h, wg_l = sb("wg_h", [P, BLOCKS * P], F16), sb("wg_l", [P, BLOCKS * P], F16)
        wd_h, wd_l = sb("wd_h", [P, BLOCKS * P], F16), sb("wd_l", [P, BLOCKS * P], F16)

        xt, h, base, x2, ot = (sb(n, [P, NT, D]) for n in ("xt", "h", "base", "x2", "ot"))
        hn, hb, t1, t2, h2 = (over_mat([NT, D]) for _ in range(5))
        xc2, t3 = t1, t2
        st, mv, st2, mv2 = sb("st", [P, NT, 6]), sb("mv", [P, NT, 2]), sb("st2", [P, NT, 6]), sb("mv2", [P, NT, 2])
        ve, rstd, ms, mse, rms, ve2, rstd2 = (sb(n, [P, NT]) for n in ("ve", "rstd", "ms", "mse", "rms", "ve2", "rstd2"))
        mhalf, eps5, eps6 = (sb(n, [P, NT]) for n in ("mhalf", "eps5", "eps6"))
        hn_h, hn_l = sb("hn_h", [P, L], F16), sb("hn_l", [P, L], F16)
        vp = sb("vp", [P, ML, L + 2 * PADL])
        z_h, z_l = sb("z_h", [P, L], F16), sb("z_l", [P, L], F16)
        cv = sb("cv", [P, ML, L])
        sbv = sb("sbv", [P, ML, L])
        s_h, s_l = over_mat([ML, L], F16), sb("s_l", [P, ML, L], F16)
        gate = sb("gate", [P, ML, L])
        gy = sb("gy", [P, ML, L])
        g_h, g_l = sb("g_h", [P, ML, L], F16), sb("g_l", [P, ML, L], F16)
        h2_h, h2_l = sb("h2_h", [P, L], F16), sb("h2_l", [P, L], F16)
        lg, pr, rp = (sb(n, [P, NT, E]) for n in ("lg", "pr", "rp"))
        cw, r1 = lg, rp
        mx = sb("mx", [P, NT, TOPK])
        sm, sme, rs = sb("sm", [P, NT]), sb("sme", [P, NT]), sb("rs", [P, NT])
        csp = sb("csp", [P, NT, STACKS, P], BF16)
        cst = sb("cst", [P, STACKS, L], BF16)
        ss = sb("ss", [INTER, L])
        ss_h, ss_l = sb("ss_h", [INTER, L], F16), sb("ss_l", [INTER, L], F16)
        ring = sb("ring", [P, 2 + RING, L])
        su, gw = ring[:, 0:2], ring[:, 2:]
        gw_h, gw_l = sb("gw_h", [P, RING, L], F16), sb("gw_l", [P, RING, L], F16)
        accs = t1.rearrange("p n d -> p (n d)")
        sq = hn
        stage = ring[:, 0:4].rearrange("p (a b) l -> p a (b l)", a=2)
        gmag, gsgn = (t[:].rearrange("p m (u j d) -> p (m u) j d", u=2, j=2) for t in (cv, sbv))
        scb = gate[:, 0, :].rearrange("p (b r) -> p b r", b=B)
        flat = gy[:].rearrange("p m l -> p (m l)")
        wf, gmat, qmat = flat[:, 0:640], flat[:, 640:768], flat[:, 768:1024]

        s = {n: sem(n) for n in (
            "ld_idf ld_vec ld_mat ld_rows ld_sd ld_sel ld_idb x_loaded out_stored out_free chunk_free "
            "pads mhalf_set ak_set silu_c scb_set mod_ps mod_half mod_set gmag_set gsgn_set gates_set "
            "fold1 fold1_sb fold2 fold3 win_f win_hi win_lo wz_f wz_hi wz_lo wab_f wab_hi wab_lo wo_f wo_hi wo_lo jb_set bz_set by_set "
            "piece_scaled piece_hi piece_lo "
            "stats aggr ve_set rstd_set t1_set h_set sq_set mse_set rms_set hn_set hnT hnT_hi hnT_lo "
            "val_ps z_ps gate_ps v_sb z_hi z_lo conv0 conv1 gate_sb silu_b s_hi s_lo y_ps gy_set g_hi g_lo o_ps "
            "hb_set hg_set base_set t2_set x2_set stats2 aggr2 ve2_set rstd2_set xc2_set h2_set h2T h2T_hi h2T_lo "
            "lg_ps lg_set pr_set mx_set rp_set cw_set sm_set sme_set rs_set cn_set c_hi r1_set c_mid r2_set c_lo cT cst_set "
            "sh_up sh_silu sh_hi sh_lo up_ready silu_done gw_done hi_done lo_done acc_ready acc_sb accT t3_set"
        ).split()}
        ld_piece = [sem("ld_piece0"), sem("ld_piece1")]

        wpiece = [wg[:, i * PIECE * P:(i + 1) * PIECE * P] for i in range(NPIECE)] + \
                 [wd[:, i * PIECE * P:(i + 1) * PIECE * P] for i in range(NPIECE)]
        xv = x.rearrange("b (n p) d -> b p n d", p=P)
        ov = out.rearrange("b (n p) d -> b p n d", p=P)

        def bc(ap, n):
            return ap.rearrange("p (t o) -> p t o", o=1).broadcast_to([P, NT, n])

        def modr(c, j, k=NT):
            return mod[:, bass.ds(c, 1), j * D:(j + 1) * D].broadcast_to([P, k, D])

        def wait_alone(eng, sem_, value):
            eng.wait_ge(s["ld_vec"], 16)
            eng.wait_ge(sem_, value)

        block = ctx.enter_context(nc.Block())

        @block.sync
        def _(sp):
            sp.dma_start(vec[:], vecs).then_inc(s["ld_vec"], 16)
            sp.dma_start(xt[:], xv[0]).then_inc(s["x_loaded"], 16)
            sp.dma_start(mat[:], mats).then_inc(s["ld_mat"], 16)
            sp.dma_start(sdf[:], sdT).then_inc(s["ld_sd"], 16)
            sp.dma_start(brow[:], rows.broadcast_to([P, E + D])).then_inc(s["ld_rows"], 16)
            sp.dma_start(sel[:], sel_c).then_inc(s["ld_sel"], 16)
            sp.dma_start(idb[:], idb_c).then_inc(s["ld_idb"], 16)
            sp.dma_start(idf[:], idf_c).then_inc(s["ld_idf"], 16)
            for i in range(2 * NPIECE):
                if i >= 2:
                    sp.wait_ge(s["piece_lo"], i - 1)
                sp.dma_start(stage[:, i % 2, :], wpiece[i]).then_inc(ld_piece[i % 2], 16)
            sp.sem_inc(s["out_free"], 1)

            def store(c):
                sp.wait_ge(s["chunk_free"], c + 2)
                sp.dma_start(ov[bass.ds(c, 1)].rearrange("a p n d -> (a p) n d"), ot[:]).then_inc(s["out_stored"], 16)
                sp.wait_ge(s["out_stored"], c * 16 + 16)
                sp.sem_inc(s["out_free"], 1)

            with sp.Fori(0, B - 1) as c:
                sp.wait_ge(s["base_set"], c + 1)
                sp.dma_start(xt[:], xv[bass.ds(c + 1, 1)].rearrange("a p n d -> (a p) n d")).then_inc(s["x_loaded"], 16)
                store(c)
            store(B - 1)

        @block.gpsimd
        def _(pool):
            g = nc.gpsimd
            for t, value in ((mhalf, -0.5), (eps5, 1e-5), (eps6, 1e-6)):
                g.memset(t[:], value).then_inc(s["mhalf_set"], 1)
            pool.wait_ge(s["mhalf_set"], 3)
            for t in (ak, a1, bm4, vp):
                g.memset(t[:], 0.0).then_inc(s["pads"], 1)
            for t in (z_h, z_l, csp):
                g.memset(t[:], 0.0).then_inc(s["pads"], 1)
            pool.wait_ge(s["mod_set"], 2 * B)
            gates = mod[:].rearrange("p b (k j d) -> p b k j d", k=2, j=3)[:, :, :, 2, :]
            pool.wait_ge(s["gmag_set"], 1)
            g.tensor_scalar(gsgn[:], gates, 0.0, None, ALU.is_ge).then_inc(s["gsgn_set"], 1)
            pool.wait_ge(s["gsgn_set"], 1)
            g.tensor_scalar(gsgn[:], gsgn[:], 2.0, -1.0, ALU.mult, ALU.add).then_inc(s["gsgn_set"], 1)
            pool.wait_ge(s["gsgn_set"], 2)
            g.tensor_scalar(gmag[:], gmag[:], 0.25, None, ALU.max).then_inc(s["gsgn_set"], 1)
            pool.wait_ge(s["gsgn_set"], 3)
            g.tensor_tensor(gates, gsgn[:], gmag[:], ALU.mult).then_inc(s["gates_set"], 1)
            pool.wait_ge(s["gates_set"], 1)

            with pool.Fori(0, B) as c:
                pool.wait_ge(s["aggr"], c + 1)
                g.tensor_tensor(ve[:], mv[:, :, 1], eps5[:], ALU.add).then_inc(s["ve_set"], 1)
                pool.wait_ge(s["ve_set"], c + 1)
                g.tensor_tensor(rstd[:], ve[:], mhalf[:], ALU.pow).then_inc(s["rstd_set"], 1)
                pool.wait_ge(s["sq_set"], c + 1)
                g.tensor_tensor(mse[:], ms[:], eps6[:], ALU.add).then_inc(s["mse_set"], 1)
                pool.wait_ge(s["mse_set"], c + 1)
                g.tensor_tensor(rms[:], mse[:], mhalf[:], ALU.pow).then_inc(s["rms_set"], 1)
                g.tensor_tensor(hb[:], h[:], outb.rearrange("p (o d) -> p o d", o=1).broadcast_to([P, NT, D]),
                                ALU.add).then_inc(s["hb_set"], 1)
                pool.wait_ge(s["hb_set"], c + 1)
                g.tensor_tensor(hb[:], hb[:], modr(c, 2), ALU.mult).then_inc(s["hg_set"], 1)
                pool.wait_ge(s["hg_set"], c + 1)
                g.tensor_tensor(base[:], hb[:], xt[:], ALU.add).then_inc(s["base_set"], 1)
                pool.wait_ge(s["s_hi"], c * ML + ML)
                g.tensor_tensor(s_l[:], sbv[:], s_h[:], ALU.subtract).then_inc(s["s_lo"], 1)
                pool.wait_ge(s["g_hi"], c * ML + ML)
                g.tensor_tensor(g_l[:], gy[:], g_h[:], ALU.subtract).then_inc(s["g_lo"], 1)
                pool.wait_ge(s["aggr2"], c + 1)
                g.tensor_tensor(ve2[:], mv2[:, :, 1], eps5[:], ALU.add).then_inc(s["ve2_set"], 1)
                pool.wait_ge(s["ve2_set"], c + 1)
                g.tensor_tensor(rstd2[:], ve2[:], mhalf[:], ALU.pow).then_inc(s["rstd2_set"], 1)
                part = [csp[:, :, :, q * ES:(q + 1) * ES] for q in range(PARTS)]

                def cols(ap):
                    return ap[:].rearrange("p t (k e) -> p t k e", k=STACKS)

                wait_alone(pool, s["cn_set"], c + 1)
                g.tensor_copy(part[0], cols(cw)).then_inc(s["c_hi"], 1)
                pool.wait_ge(s["c_hi"], c + 1)
                g.tensor_tensor(cols(r1), cols(cw), part[0], ALU.subtract).then_inc(s["r1_set"], 1)
                wait_alone(pool, s["r1_set"], c + 1)
                g.tensor_copy(part[1], cols(r1)).then_inc(s["c_mid"], 1)
                pool.wait_ge(s["c_mid"], c + 1)
                g.tensor_tensor(part[2], cols(r1), part[1], ALU.subtract).then_inc(s["c_lo"], 1)

        @block.scalar
        def _(act):
            a = nc.scalar.activation
            act.wait_ge(s["ld_vec"], 16)
            a(sct[:], v("cT", 0, B), ACT.Silu).then_inc(s["silu_c"], 1)
            act.wait_ge(s["win_f"], 1)
            a(win_h[:], wf[:, 0:2 * DI], ACT.Copy).then_inc(s["win_hi"], 1)
            for b in range(B):
                act.wait_ge(s["mod_ps"], 2 * b + 1)
                a(mod[:, b, 0:512], pa[:], ACT.Copy).then_inc(s["mod_half"], 1)
                act.wait_ge(s["mod_ps"], 2 * b + 2)
                a(mod[:, b, 512:768], pb[:, 0:256], ACT.Copy).then_inc(s["mod_half"], 1)
            act.wait_ge(s["mod_set"], 2 * B)
            a(gmag[:], mod[:].rearrange("p b (k j d) -> p b k j d", k=2, j=3)[:, :, :, 2, :], ACT.Abs)\
                .then_inc(s["gmag_set"], 1)
            act.wait_ge(s["wz_f"], 1)
            a(wz_h[:], wf[:, 512:640], ACT.Copy).then_inc(s["wz_hi"], 1)
            act.wait_ge(s["ld_mat"], 16)
            a(wo_h[:].rearrange("p m d -> p (m d)"), m("outT"), ACT.Copy, scale=WS).then_inc(s["wo_hi"], 1)
            a(wr_h[:], m("rT"), ACT.Copy, scale=ES_SCALE).then_inc(s["wo_hi"], 1)
            a(sg_h[:], m("sgT"), ACT.Copy, scale=ES_SCALE).then_inc(s["wo_hi"], 1)
            act.wait_ge(s["ld_sd"], 16)
            a(sd_h[:], sdf[:], ACT.Copy, scale=ES_SCALE).then_inc(s["wo_hi"], 1)
            act.wait_ge(s["fold3"], 1)
            a(wa_h[:], pa[:, 0:DI], ACT.Copy).then_inc(s["wab_hi"], 1)
            act.wait_ge(s["fold3"], 2)
            a(wb_h[:].rearrange("p m o -> p (m o)"), pb[:], ACT.Copy, scale=WS).then_inc(s["wab_hi"], 1)
            for i in range(2 * NPIECE):
                dst = (wg_h if i < NPIECE else wd_h)[:, i % NPIECE * PIECE * P:(i % NPIECE + 1) * PIECE * P]
                act.wait_ge(ld_piece[i % 2], 16 * (i // 2 + 1))
                a(dst, stage[:, i % 2, :], ACT.Copy, scale=ES_SCALE).then_inc(s["piece_hi"], 1)

            def silu(c, b, k):
                act.wait_ge(s["up_ready"], c * BLOCKS + b + 1)
                a(su[:, k % 2, :], up_ps[k % 2][:], ACT.Silu, scale=1.0 / ES_SCALE).then_inc(s["silu_done"], 1)

            def high(c, b, k):
                act.wait_ge(s["gw_done"], c * BLOCKS + b + 1)
                a(gw_h[:, k % RING, :], gw[:, k % RING, :], ACT.Copy).then_inc(s["hi_done"], 1)

            with act.Fori(0, B) as c:
                for n in range(NT):
                    act.wait_ge(s["h_set"], c * NT + n + 1)
                    last = a(sq[:, n, :], h[:, n, :], ACT.Square, scale=D ** -0.5, accum_out=ms[:, n:n + 1])
                last.then_inc(s["sq_set"], 1)
                act.wait_ge(s["hnT"], c + 1)
                a(hn_h[:], pa[:], ACT.Copy).then_inc(s["hnT_hi"], 1)
                for k in range(ML):
                    act.wait_ge(s["val_ps"], c * ML + k + 1)
                    a(vp[:, k, PADL:PADL + L], (pb, pc)[k][:], ACT.Identity, bias=v("in_b", ML + k),
                      scale=1.0 / WS).then_inc(s["v_sb"], 1)
                act.wait_ge(s["z_ps"], c + 1)
                for k in range(DC):
                    lo, hi = max(0, 1 - k), min(L, L + 1 - k)
                    q = slice(32 * k, 32 * k + 32)
                    a(z_h[q, lo:hi], pa[q, lo + k - 1:hi + k - 1], ACT.Identity, bias=bz[q, 0:1])\
                        .then_inc(s["z_hi"], 1)
                for k in range(ML):
                    act.wait_ge(s["gate_ps"], c * ML + k + 1)
                    a(gate[:, k, :], (pb, pc)[k][:], ACT.Sigmoid, bias=v("in_b", k), scale=1.0 / WS)\
                        .then_inc(s["gate_sb"], 1)
                for k in range(ML):
                    act.wait_ge(s[f"conv{k}"], c * KS + KS)
                    a(sbv[:, k, :], cv[:, k, :], ACT.Silu).then_inc(s["silu_b"], 1)
                    act.wait_ge(s["silu_b"], c * ML + k + 1)
                    a(s_h[:, k, :], sbv[:, k, :], ACT.Copy).then_inc(s["s_hi"], 1)
                for k in range(ML):
                    act.wait_ge(s["gy_set"], c * ML + k + 1)
                    a(g_h[:, k, :], gy[:, k, :], ACT.Copy).then_inc(s["g_hi"], 1)
                act.wait_ge(s["h2T"], c + 1)
                a(h2_h[:], pa[:], ACT.Copy).then_inc(s["h2T_hi"], 1)
                act.wait_ge(s["lg_set"], c * 2 + 2)
                a(pr[:], lg[:], ACT.Sigmoid).then_inc(s["pr_set"], 1)
                act.wait_ge(s["sh_up"], c + 1)
                a(ss[:], pa[0:INTER, :], ACT.Silu, scale=1.0 / ES_SCALE).then_inc(s["sh_silu"], 1)
                act.wait_ge(s["sh_silu"], c + 1)
                a(ss_h[:], ss[:], ACT.Copy).then_inc(s["sh_hi"], 1)
                silu(c, 0, 0)
                for k in range(1, RING):
                    silu(c, k, k)
                    high(c, k - 1, k - 1)
                with act.Fori(1, GROUPS) as gi:
                    for k in range(RING):
                        silu(c, gi * RING + k, k)
                        high(c, gi * RING + (k - 1), k - 1)
                high(c, BLOCKS - 1, RING - 1)
                act.wait_ge(s["acc_ready"], c + 1)
                a(accs[:], acc_ps[:], ACT.Copy, scale=1.0 / ES_SCALE).then_inc(s["acc_sb"], 1)

        @block.vector
        def _(dve):
            e = nc.vector
            dve.wait_ge(s["ld_vec"], 16)
            dve.wait_ge(s["pads"], 7)
            for mm in range(ML):
                for k in range(DC):
                    e.tensor_scalar(ak[:, mm, 32 * k:32 * k + DS], v("A", mm * DS, DS), v("dwa_k", mm * DC + k), None,
                                    ALU.mult).then_inc(s["ak_set"], 1)
                    e.tensor_copy(bm4[:, mm, 32 * k:32 * k + DS], v("BmT", mm * DS, DS)).then_inc(s["ak_set"], 1)
                e.tensor_copy(a1[:, mm, 32:32 + DS], v("A", mm * DS, DS)).then_inc(s["ak_set"], 1)
            dve.wait_ge(s["silu_c"], 1)
            e.tensor_copy(scb[:], sct[:].rearrange("p (b o) -> p b o", o=1).broadcast_to([P, B, P]))\
                .then_inc(s["scb_set"], 1)
            dve.wait_ge(s["ld_mat"], 16)
            e.tensor_scalar(wf[:, 0:2 * DI], m("in_wT"), v("norm_w"), WS, ALU.mult, ALU.mult).then_inc(s["win_f"], 1)
            dve.wait_ge(s["win_hi"], 1)
            e.tensor_tensor(win_l[:], wf[:, 0:2 * DI], win_h[:], ALU.subtract).then_inc(s["win_lo"], 1)
            for b in range(B):
                for j in (1, 4):
                    dve.wait_ge(s["mod_half"], 2 * b + (2 if j == 4 else 1))
                    r = mod[:, b, j * D:(j + 1) * D]
                    e.tensor_scalar(r, r, 1.0, None, ALU.add).then_inc(s["mod_set"], 1)
            dve.wait_ge(s["fold1"], 1)
            e.tensor_copy(gmat[:], pc[:, 0:P]).then_inc(s["fold1_sb"], 1)
            e.tensor_copy(qmat[:], pc[:, P:P + DI]).then_inc(s["fold1_sb"], 1)
            e.tensor_tensor(jb[:], pc[:, 384:385], v("hb_b"), ALU.add).then_inc(s["jb_set"], 1)
            dve.wait_ge(s["fold2"], 1)
            e.tensor_scalar(wf[:, 512:640], acc_ps[:, 0:P], v("norm_w"), WS, ALU.mult, ALU.mult)\
                .then_inc(s["wz_f"], 1)
            e.tensor_scalar(bz[:], acc_ps[:, 128:129], WS, None, ALU.mult).then_inc(s["bz_set"], 1)
            dve.wait_ge(s["wz_hi"], 1)
            e.tensor_tensor(wz_l[:], wf[:, 512:640], wz_h[:], ALU.subtract).then_inc(s["wz_lo"], 1)
            for i, (hi, src, lo) in enumerate(((wo_h[:].rearrange("p m d -> p (m d)"), m("outT"),
                                                wo_l[:].rearrange("p m d -> p (m d)")),
                                               (wr_h[:], m("rT"), wr_l[:]), (sg_h[:], m("sgT"), sg_l[:]),
                                               (sd_h[:], sdf[:], sd_l[:]))):
                dve.wait_ge(s["wo_hi"], i + 1)
                e.scalar_tensor_tensor(out=lo, in0=src, scalar=WS if i == 0 else ES_SCALE, in1=hi, op0=ALU.mult,
                                       op1=ALU.subtract).then_inc(s["wo_lo"], 1)
            dve.wait_ge(s["wab_hi"], 1)
            e.tensor_tensor(wa_l[:], pa[:, 0:DI], wa_h[:], ALU.subtract).then_inc(s["wab_lo"], 1)
            dve.wait_ge(s["wab_hi"], 2)
            e.scalar_tensor_tensor(out=wb_l[:].rearrange("p m o -> p (m o)"), in0=pb[:], scalar=WS,
                                   in1=wb_h[:].rearrange("p m o -> p (m o)"), op0=ALU.mult,
                                   op1=ALU.subtract).then_inc(s["wab_lo"], 1)
            e.tensor_tensor(by[:], pa[:, 256:256 + ML], v("fuse_b", 0, ML), ALU.add).then_inc(s["by_set"], 1)
            dve.wait_ge(s["by_set"], 1)
            e.tensor_scalar(by[:], by[:], WS, None, ALU.mult).then_inc(s["by_set"], 1)
            dve.wait_ge(s["by_set"], 2)
            for i in range(2 * NPIECE):
                at = slice(i % NPIECE * PIECE * P, (i % NPIECE + 1) * PIECE * P)
                hi, lo = ((wg_h, wg_l) if i < NPIECE else (wd_h, wd_l))
                dve.wait_ge(s["piece_hi"], i + 1)
                e.scalar_tensor_tensor(out=lo[:, at], in0=stage[:, i % 2, :], scalar=ES_SCALE, in1=hi[:, at],
                                       op0=ALU.mult, op1=ALU.subtract).then_inc(s["piece_lo"], 1)
            dve.wait_ge(s["gates_set"], 1)
            dve.wait_ge(s["ld_rows"], 16)
            e.sem_inc(s["chunk_free"], 1)

            def weigh(c, b, k):
                dve.wait_ge(s["silu_done"], c * BLOCKS + b + 1)
                e.tensor_tensor(gw[:, k % RING, :], cb_ps[k % 2][:], su[:, k % 2, :], ALU.mult)\
                    .then_inc(s["gw_done"], 1)

            def low(c, b, k):
                dve.wait_ge(s["hi_done"], c * BLOCKS + b + 1)
                e.tensor_tensor(gw_l[:, k % RING, :], gw[:, k % RING, :], gw_h[:, k % RING, :], ALU.subtract)\
                    .then_inc(s["lo_done"], 1)

            with dve.Fori(0, B) as c:
                dve.wait_ge(s["chunk_free"], c + 1)
                dve.wait_ge(s["x_loaded"], c * 16 + 16)
                for n in range(NT):
                    last = e.bn_stats(st[:, n, :], xt[:, n, :])
                last.then_inc(s["stats"], 1)
                wait_alone(dve, s["stats"], c + 1)
                for n in range(NT):
                    last = e.bn_aggr(mv[:, n, :], st[:, n, :])
                last.then_inc(s["aggr"], 1)
                dve.wait_ge(s["aggr"], c + 1)
                ca, sa = (mod[:, bass.ds(c, 1), j * D:(j + 1) * D].rearrange("p a d -> p (a d)") for j in (1, 0))
                for n in range(NT):
                    e.scalar_tensor_tensor(out=t1[:, n, :], in0=xt[:, n, :], scalar=mv[:, n, 0:1], in1=ca,
                                           op0=ALU.subtract, op1=ALU.mult).then_inc(s["t1_set"], 1)
                dve.wait_ge(s["rstd_set"], c + 1)
                for n in range(NT):
                    dve.wait_ge(s["t1_set"], c * NT + n + 1)
                    e.scalar_tensor_tensor(out=h[:, n, :], in0=t1[:, n, :], scalar=rstd[:, n:n + 1], in1=sa,
                                           op0=ALU.mult, op1=ALU.add).then_inc(s["h_set"], 1)
                dve.wait_ge(s["rms_set"], c + 1)
                e.tensor_tensor(hn[:], h[:], bc(rms[:], D), ALU.mult).then_inc(s["hn_set"], 1)
                dve.wait_ge(s["hnT_hi"], c + 1)
                e.tensor_tensor(hn_l[:], pa[:], hn_h[:], ALU.subtract).then_inc(s["hnT_lo"], 1)
                for k in range(DC):
                    lo, hi = max(0, 1 - k), min(L, L + 1 - k)
                    q = slice(32 * k, 32 * k + 32)
                    dve.wait_ge(s["z_hi"], c * DC + k + 1)
                    e.scalar_tensor_tensor(out=z_l[q, lo:hi], in0=pa[q, lo + k - 1:hi + k - 1], scalar=bz[q, 0:1],
                                           in1=z_h[q, lo:hi], op0=ALU.add, op1=ALU.subtract).then_inc(s["z_lo"], 1)
                for k in range(KS):
                    for mm in range(ML):
                        src = vp[:, mm, k:k + L]
                        if k == 0:
                            dve.wait_ge(s["v_sb"], c * ML + mm + 1)
                            e.tensor_scalar(cv[:, mm, :], src, v("sym_k", mm * KS), v("sym_b", mm), ALU.mult,
                                            ALU.add).then_inc(s[f"conv{mm}"], 1)
                        else:
                            dve.wait_ge(s[f"conv{mm}"], c * KS + k)
                            e.scalar_tensor_tensor(out=cv[:, mm, :], in0=src, scalar=v("sym_k", mm * KS + k),
                                                   in1=cv[:, mm, :], op0=ALU.mult, op1=ALU.add)\
                                .then_inc(s[f"conv{mm}"], 1)
                dve.wait_ge(s["gate_sb"], c * ML + ML)
                for k in range(ML):
                    dve.wait_ge(s["y_ps"], c * ML + k + 1)
                    e.scalar_tensor_tensor(out=gy[:, k, :], in0=(pb, pc)[k][:], scalar=by[:, k:k + 1],
                                           in1=gate[:, k, :], op0=ALU.add, op1=ALU.mult).then_inc(s["gy_set"], 1)
                dve.wait_ge(s["o_ps"], c + 1)
                e.scalar_tensor_tensor(out=t2[:], in0=pa[:].rearrange("p (n d) -> p n d", d=D),
                                       scalar=1.0 / (WS * WS), in1=modr(c, 2), op0=ALU.mult, op1=ALU.mult)\
                    .then_inc(s["t2_set"], 1)
                dve.wait_ge(s["t2_set"], c + 1)
                dve.wait_ge(s["base_set"], c + 1)
                e.tensor_tensor(x2[:], t2[:], base[:], ALU.add).then_inc(s["x2_set"], 1)
                dve.wait_ge(s["x2_set"], c + 1)
                for n in range(NT):
                    last = e.bn_stats(st2[:, n, :], x2[:, n, :])
                last.then_inc(s["stats2"], 1)
                wait_alone(dve, s["stats2"], c + 1)
                for n in range(NT):
                    last = e.bn_aggr(mv2[:, n, :], st2[:, n, :])
                last.then_inc(s["aggr2"], 1)
                dve.wait_ge(s["aggr2"], c + 1)
                cb, sbb = (mod[:, bass.ds(c, 1), j * D:(j + 1) * D].rearrange("p a d -> p (a d)") for j in (4, 3))
                for n in range(NT):
                    e.scalar_tensor_tensor(out=xc2[:, n, :], in0=x2[:, n, :], scalar=mv2[:, n, 0:1], in1=cb,
                                           op0=ALU.subtract, op1=ALU.mult).then_inc(s["xc2_set"], 1)
                dve.wait_ge(s["rstd2_set"], c + 1)
                for n in range(NT):
                    dve.wait_ge(s["xc2_set"], c * NT + n + 1)
                    e.scalar_tensor_tensor(out=h2[:, n, :], in0=xc2[:, n, :], scalar=rstd2[:, n:n + 1], in1=sbb,
                                           op0=ALU.mult, op1=ALU.add).then_inc(s["h2_set"], 1)
                dve.wait_ge(s["h2T_hi"], c + 1)
                e.tensor_tensor(h2_l[:], pa[:], h2_h[:], ALU.subtract).then_inc(s["h2T_lo"], 1)
                for k in range(2):
                    dve.wait_ge(s["lg_ps"], c * 2 + k + 1)
                    e.scalar_tensor_tensor(
                        out=lg[:, 2 * k:2 * k + 2, :],
                        in0=(pb, pc)[k][:, 0:2 * E].rearrange("p (n e) -> p n e", n=2), scalar=1.0 / ES_SCALE,
                        in1=ebias.rearrange("p (o e) -> p o e", o=1).broadcast_to([P, 2, E]), op0=ALU.mult,
                        op1=ALU.add).then_inc(s["lg_set"], 1)
                wait_alone(dve, s["pr_set"], c + 1)
                for n in range(NT):
                    e.max(mx[:, n, :], pr[:, n, :]).then_inc(s["mx_set"], 1)
                for n in range(NT):
                    wait_alone(dve, s["mx_set"], c * NT + n + 1)
                    e.match_replace(rp[:, n, :], mx[:, n, :], pr[:, n, :], 0.0).then_inc(s["rp_set"], 1)
                e.tensor_reduce(sm[:], mx[:], AX.X, ALU.add).then_inc(s["sm_set"], 1)
                dve.wait_ge(s["rp_set"], c * NT + NT)
                e.tensor_tensor(cw[:], pr[:], rp[:], ALU.subtract).then_inc(s["cw_set"], 1)
                dve.wait_ge(s["sm_set"], c + 1)
                e.tensor_scalar(sme[:], sm[:], 1e-9, 1.0 / ROUTED_SCALE, ALU.add, ALU.mult).then_inc(s["sme_set"], 1)
                dve.wait_ge(s["sme_set"], c + 1)
                e.reciprocal(rs[:], sme[:]).then_inc(s["rs_set"], 1)
                dve.wait_ge(s["rs_set"], c + 1)
                dve.wait_ge(s["cw_set"], c + 1)
                e.tensor_tensor(cw[:], cw[:], bc(rs[:], E), ALU.mult).then_inc(s["cn_set"], 1)
                dve.wait_ge(s["sh_hi"], c + 1)
                e.tensor_tensor(ss_l[:], ss[:], ss_h[:], ALU.subtract).then_inc(s["sh_lo"], 1)
                for k in range(2):
                    dve.wait_ge(s["cT"], c * 2 + k + 1)
                    e.tensor_copy(cst[:, 2 * k:2 * k + 2, :].rearrange("p k t -> p (k t)"),
                                  (pb, pc)[k][:].bitcast(BF16)).then_inc(s["cst_set"], 1)
                weigh(c, 0, 0)
                for k in range(1, RING):
                    weigh(c, k, k)
                    low(c, k - 1, k - 1)
                with dve.Fori(1, GROUPS) as gi:
                    for k in range(RING):
                        weigh(c, gi * RING + k, k)
                        low(c, gi * RING + (k - 1), k - 1)
                low(c, BLOCKS - 1, RING - 1)
                dve.wait_ge(s["accT"], c + 1)
                e.tensor_tensor(t3[:], pa[:].rearrange("p (n d) -> p n d", d=D), modr(c, 5), ALU.mult)\
                    .then_inc(s["t3_set"], 1)
                dve.wait_ge(s["t3_set"], c + 1)
                dve.wait_ge(s["out_free"], c + 1)
                e.tensor_tensor(ot[:], t3[:], x2[:], ALU.add).then_inc(s["chunk_free"], 1)

        @block.tensor
        def _(pe):
            mm = nc.tensor.matmul

            def split(dst, lhs, rhs, start=True, stop=True):
                (lh, ll), (rh, rl) = lhs, rhs
                mm(dst, lh, rh, start=start, stop=False)
                mm(dst, ll, rh, start=False, stop=False)
                return mm(dst, lh, rl, start=False, stop=stop)

            pe.wait_ge(s["ld_mat"], 16)
            pe.wait_ge(s["scb_set"], 1)
            for b in range(B):
                if b:
                    pe.wait_ge(s["mod_half"], 2 * b)
                mm(pa[:], scb[:, b, :], m("wmod", 0, 512)).then_inc(s["mod_ps"], 1)
                mm(pb[:, 0:256], scb[:, b, :], m("wmod", 512, 256)).then_inc(s["mod_ps"], 1)
            pe.wait_ge(s["ak_set"], ML * (2 * DC + 1))
            for k in range(ML):
                mm(pc[:, 0:P], m("haT", k * P, P), bm4[:, k, :], start=(k == 0), stop=(k == ML - 1))
            for k in range(ML):
                mm(pc[:, P:P + DI], m("hbT", k * P, P), m("pw", k * DI, DI), start=(k == 0), stop=(k == ML - 1))
            for k in range(ML):
                last = mm(pc[:, 384:385], m("hbT", k * P, P), v("pw_b", k), start=(k == 0), stop=(k == ML - 1))
            last.then_inc(s["fold1"], 1)
            for k in range(ML):
                mm(acc_ps[:, 0:P], m("inv", k * D, D), ak[:, k, :], start=(k == 0), stop=(k == ML - 1))
            for k in range(ML):
                mm(acc_ps[:, 128:129], ak[:, k, :], v("in_b", ML + k), start=(k == 0), stop=False)
            for k in range(ML):
                last = mm(acc_ps[:, 128:129], a1[:, k, :], v("dwa_b", k), start=False, stop=(k == ML - 1))
            last.then_inc(s["fold2"], 1)
            pe.wait_ge(s["fold1_sb"], 2)
            pe.wait_ge(s["jb_set"], 1)
            pe.wait_ge(s["mod_half"], 2 * B)
            mm(pa[:, 0:DI], gmat[:], m("fuseT", 0, DI))
            for k in range(ML):
                mm(pa[:, 256 + k:257 + k], m("fuseT", k * P, P), v("ha_b"), start=True, stop=False)
                last = mm(pa[:, 256 + k:257 + k], m("fuseT", DI + k * P, P), jb[:], start=False, stop=True)
            last.then_inc(s["fold3"], 1)
            for k in range(ML):
                last = mm(pb[:, k * DI:(k + 1) * DI], qmat[:, k * P:(k + 1) * P], m("fuseT", DI, DI))
            last.then_inc(s["fold3"], 1)
            pe.wait_ge(s["win_lo"], 1)
            pe.wait_ge(s["wz_lo"], 1)
            pe.wait_ge(s["wo_lo"], 4)
            pe.wait_ge(s["wab_lo"], 2)
            pe.wait_ge(s["by_set"], 1)
            pe.wait_ge(s["piece_lo"], 2 * NPIECE)
            pe.wait_ge(s["ld_idb"], 16)
            pe.wait_ge(s["ld_idf"], 16)
            pe.wait_ge(s["ld_sel"], 16)

            hnT = (hn_h[:], hn_l[:])
            h2T = (h2_h[:], h2_l[:])

            def up(c, b, gi, k, wait=True):
                if wait:
                    pe.wait_ge(s["gw_done"], c * BLOCKS + b - 1)
                mm(cb_ps[k % 2][:], sel[:, bass.ds(gi * P, P)], cst[:, k, :])
                w = bass.ds(b * P, P)
                split(up_ps[k % 2][:], (wg_h[:, w], wg_l[:, w]), h2T).then_inc(s["up_ready"], 1)

            def down(c, b, k, stop=False):
                pe.wait_ge(s["lo_done"], c * BLOCKS + b + 1)
                w = bass.ds(b * P, P)
                return split(acc_ps[:], (wd_h[:, w], wd_l[:, w]), (gw_h[:, k % RING, :], gw_l[:, k % RING, :]),
                             start=False, stop=stop)

            with pe.Fori(0, B) as c:
                pe.wait_ge(s["chunk_free"], c + 1)
                pe.wait_ge(s["hn_set"], c + 1)
                for n in range(NT):
                    last = nc.tensor.transpose(pa[:, n * P:(n + 1) * P], hn[:, n, :], idf[:])
                last.then_inc(s["hnT"], 1)
                pe.wait_ge(s["hnT_lo"], c + 1)
                for k in range(ML):
                    w = slice(DI + k * P, DI + (k + 1) * P)
                    split((pb, pc)[k][:], (win_h[:, w], win_l[:, w]), hnT).then_inc(s["val_ps"], 1)
                split(pa[:], (wz_h[:], wz_l[:]), hnT).then_inc(s["z_ps"], 1)
                for k in range(ML):
                    pe.wait_ge(s["v_sb"], c * ML + k + 1)
                    w = slice(k * P, (k + 1) * P)
                    split((pb, pc)[k][:], (win_h[:, w], win_l[:, w]), hnT).then_inc(s["gate_ps"], 1)
                pe.wait_ge(s["z_lo"], c * DC + DC)
                pe.wait_ge(s["gate_sb"], c * ML + ML)
                for k in range(ML):
                    w = slice(k * P, (k + 1) * P)
                    split((pb, pc)[k][:], (wa_h[:, w], wa_l[:, w]), (z_h[:], z_l[:]), stop=False)
                pe.wait_ge(s["s_lo"], c + 1)
                for k in range(ML):
                    w = slice(k * P, (k + 1) * P)
                    for i in range(ML):
                        last = split((pb, pc)[k][:], (wb_h[:, i, w], wb_l[:, i, w]), (s_h[:, i, :], s_l[:, i, :]),
                                     start=False, stop=(i == ML - 1))
                    last.then_inc(s["y_ps"], 1)
                pe.wait_ge(s["g_lo"], c + 1)
                for n in range(NT):
                    t = slice(n * P, (n + 1) * P)
                    for i in range(ML):
                        last = split(pa[:, n * D:(n + 1) * D], (g_h[:, i, t], g_l[:, i, t]),
                                     (wo_h[:, i, :], wo_l[:, i, :]), start=(i == 0), stop=(i == ML - 1))
                last.then_inc(s["o_ps"], 1)
                pe.wait_ge(s["h2_set"], c * NT + NT)
                for n in range(NT):
                    last = nc.tensor.transpose(pa[:, n * P:(n + 1) * P], h2[:, n, :], idf[:])
                last.then_inc(s["h2T"], 1)
                pe.wait_ge(s["h2T_lo"], c + 1)
                for n in range(NT):
                    t = slice(n * P, (n + 1) * P)
                    last = split((pb, pc)[n // 2][:, n % 2 * E:(n % 2 + 1) * E], (h2_h[:, t], h2_l[:, t]),
                                 (wr_h[:], wr_l[:]))
                    if n % 2:
                        last.then_inc(s["lg_ps"], 1)
                split(pa[0:INTER, :], (sg_h[:], sg_l[:]), h2T).then_inc(s["sh_up"], 1)
                pe.wait_ge(s["c_lo"], c + 1)
                for k in range(STACKS):
                    for n in range(NT):
                        last = nc.tensor.transpose(
                            (pb, pc)[k // 2][:].bitcast(BF16)[:, k % 2 * L + n * P:k % 2 * L + (n + 1) * P],
                            csp[:, n, k, :], idb[:])
                    if k % 2:
                        last.then_inc(s["cT"], 1)
                pe.wait_ge(s["sh_lo"], c + 1)
                split(acc_ps[:], (sd_h[:], sd_l[:]), (ss_h[:], ss_l[:]), stop=False)
                pe.wait_ge(s["cst_set"], c * 2 + 2)
                for k in range(RING):
                    up(c, k, 0, k, wait=k >= 2)
                    if k >= LAG:
                        down(c, k - LAG, k - LAG)
                with pe.Fori(1, GROUPS) as gi:
                    for k in range(RING):
                        up(c, gi * RING + k, gi, k)
                        down(c, gi * RING + (k - LAG), (k - LAG) % RING)
                for k in range(RING - LAG, RING):
                    last = down(c, BLOCKS - RING + k, k, stop=(k == RING - 1))
                last.then_inc(s["acc_ready"], 1)
                pe.wait_ge(s["acc_sb"], c + 1)
                for n in range(NT):
                    last = nc.tensor.transpose(pa[:, n * P:(n + 1) * P], accs[:, n * P:(n + 1) * P], idf[:])
                last.then_inc(s["accT"], 1)


_W = "L0_attn_"
_F = "L0_ffn_"


def kernel(**inputs):
    import ml_dtypes
    import numpy as np
    import concourse.bacc as bacc
    from concourse.bass_utils import run_bass_kernel_spmd

    a = {k: np.asarray(t) for k, t in inputs.items()}

    def blocks(t):
        return np.concatenate(np.split(t.reshape(t.shape[0], -1), t.shape[0] // P), 1)

    w = {k[len(_W):]: t for k, t in a.items() if k.startswith(_W)}
    f = {k[len(_F):]: t for k, t in a.items() if k.startswith(_F)}
    vecs = np.concatenate([blocks(t) for t in (
        w["norm_w"], w["in_b"], w["dwa_b"], w["sym_b"], w["pw_b"], w["fuse_b"], w["ha_b"], w["hb_b"],
        w["dwa_k"], w["sym_k"], w["A"], w["Bm"].T, a["L0_c"].T)], 1)
    mats = np.concatenate([blocks(t) for t in (
        a["L0_wmod"], w["in_w"].T, w["in_w"][DI:], w["ha_w"].T, w["hb_w"].T, w["pw_w"], w["fuse_w"].T, w["out_w"].T,
        f["router_w"].T, f["w_gate_shared"].T)], 1)
    rows = np.concatenate([f["expert_bias"], w["out_b"]])[None]
    wg = f["w_gate"].reshape(STACKS, GROUPS, 2 * INTER, D).transpose(3, 1, 0, 2).reshape(D, BLOCKS * P)
    wd = f["w_down"].reshape(STACKS, GROUPS, 2, D, INTER).transpose(2, 4, 1, 0, 3).reshape(P, BLOCKS * D)
    sel = np.zeros((P, GROUPS * 2, INTER), ml_dtypes.bfloat16)
    for q in range(PARTS):
        sel[q * ES + np.arange(ES), np.arange(ES)] = 1
    arrays = {"x": w["x"], "vecs": vecs, "mats": mats, "sdT": f["w_down_shared"].T, "rows": rows,
              "sel": sel.reshape(P, GROUPS * P), "idb": np.eye(P, dtype=ml_dtypes.bfloat16),
              "idf": np.eye(P, dtype=np.float32), "wg": wg, "wd": wd}
    arrays = {f"{k}_dram": np.ascontiguousarray(t) for k, t in arrays.items()}
    nc = bacc.Bacc("TRN2", target_bir_lowering=False, num_devices=1)
    args = [nc.dram_tensor(k, t.shape, mybir.dt.from_np(t.dtype), kind="ExternalInput").ap()
            for k, t in arrays.items()]
    out = nc.dram_tensor("out_dram", (B, L, D), F32, kind="ExternalOutput").ap()
    build(nc, *args, out)
    r = run_bass_kernel_spmd(nc, [arrays], core_ids=[0])
    return r.results[0]["out_dram"]
```

```python
from contextlib import ExitStack

import concourse.bass as bass
from concourse import mybir

F32 = mybir.dt.float32
F16 = mybir.dt.float16
BF16 = mybir.dt.bfloat16
ALU = mybir.AluOpType
ACT = mybir.ActivationFunctionType
AX = mybir.AxisListType

P = 128
B, L, D = 4, 512, 128
DI = 2 * D
ML = DI // P
DS, DC = 16, 4
KS = 2 * DC + 1
PADL = KS // 2
NT = L // P
E, TOPK, INTER = 160, 8, 64
ROUTED_SCALE = 2.5
BLOCKS = E // 2
BODY = 8
GROUPS = BLOCKS // 4
LAG = 5
URING = 4
SLOTB = 2
CSLOTS = 4
LOADS = BLOCKS // SLOTB
WS = 16.0
ES_SCALE = 64.0
PIECE = 8
NPIECE = BLOCKS // PIECE

V = {}
_at = 0
for _n, _w in (("norm_w", 1), ("in_b", 4), ("dwa_b", ML), ("sym_b", ML), ("pw_b", ML), ("fuse_b", ML),
               ("ha_b", 1), ("hb_b", 1), ("dwa_k", ML * DC), ("sym_k", ML * KS), ("A", ML * DS), ("BmT", ML * DS),
               ("cT", B)):
    V[_n] = (_at, _w)
    _at += _w
NV = _at
M = {}
_at = 0
for _n, _w in (("wmod", 6 * D), ("in_wT", 2 * DI), ("inv", ML * D), ("haT", ML * P), ("hbT", ML * P),
               ("pw", ML * DI), ("fuseT", ML * DI), ("outT", ML * D), ("rT", E), ("sgT", INTER)):
    M[_n] = (_at, _w)
    _at += _w
NM = _at


def build(nc, x, vecs, mats, sdT, rows, idf_c, wg, wd, out):
    c_dram = nc.dram_tensor("combine", (B, E, L), F32, kind="Internal").ap()
    with ExitStack() as ctx:
        def sb(name, shape, dt=F32):
            return ctx.enter_context(nc.sbuf_tensor(name, shape, dt))

        def sem(name):
            return ctx.enter_context(nc.semaphore(name))

        bank = [ctx.enter_context(nc.psum_tensor(f"bank{i}", [P, 512], F32)) for i in range(8)]
        up_ps, acc_ps = bank[0:URING], bank[4]
        pa, pb, pc = bank[5], bank[6], bank[7]

        vec = sb("vec", [P, NV])
        mat = sb("mat", [P, NM])
        idf = sb("idf", [P, P])
        room = [0]

        def over_mat(shape, dt=F32):
            words = shape[0] * shape[1] * (2 if dt == F16 else 4) // 4
            ap = mat[:, room[0]:room[0] + words]
            room[0] += words
            assert room[0] <= NM
            ap = ap if dt == F32 else ap.bitcast(dt)
            return ap.rearrange("p (a b) -> p a b", a=shape[0])

        sdf = sb("sdf", [INTER, P])
        brow = sb("brow", [P, E + D])

        def v(name, i=0, n=1):
            at = V[name][0] + i
            return vec[:, at:at + n]

        def m(name, i=0, n=None):
            at, w = M[name]
            return mat[:, at + i:at + (w if n is None else i + n)]

        ebias, outb = brow[:, 0:E], brow[:, E:E + D]

        win_h, win_l = sb("win_h", [P, 2 * DI], F16), sb("win_l", [P, 2 * DI], F16)
        wz_h, wz_l = sb("wz_h", [P, P], F16), sb("wz_l", [P, P], F16)
        wa_h, wa_l = sb("wa_h", [P, DI], F16), sb("wa_l", [P, DI], F16)
        wb_h, wb_l = sb("wb_h", [P, ML, DI], F16), sb("wb_l", [P, ML, DI], F16)
        wo_h, wo_l = sb("wo_h", [P, ML, D], F16), sb("wo_l", [P, ML, D], F16)
        wr_h, wr_l = sb("wr_h", [P, E], F16), sb("wr_l", [P, E], F16)
        sg_h, sg_l = sb("sg_h", [P, INTER], F16), sb("sg_l", [P, INTER], F16)
        sd_h, sd_l = sb("sd_h", [INTER, P], F16), sb("sd_l", [INTER, P], F16)
        cbr = sb("cbr", [P, CSLOTS, SLOTB * L])
        jb, bz, by = sb("jb", [P, 1]), sb("bz", [P, 1]), sb("by", [P, ML])
        sct = sb("sct", [P, B])
        mod = sb("mod", [P, B, 6 * D])

        wg_h, wg_l = sb("wg_h", [P, BLOCKS * P], F16), sb("wg_l", [P, BLOCKS * P], F16)
        wd_h, wd_l = sb("wd_h", [P, BLOCKS * P], F16), sb("wd_l", [P, BLOCKS * P], F16)

        xt, h, x2, xf, ot = (sb(n, [P, NT, D]) for n in ("xt", "h", "x2", "xf", "ot"))
        base = xt
        hn, hb, t1, t2, h2 = (over_mat([NT, D]) for _ in range(5))
        xc2, t3 = t1, t2
        st, mv, st2, mv2 = sb("st", [P, NT, 6]), sb("mv", [P, NT, 2]), sb("st2", [P, NT, 6]), sb("mv2", [P, NT, 2])
        ve, rstd, ms, mse, rms, ve2, rstd2 = (sb(n, [P, NT]) for n in ("ve", "rstd", "ms", "mse", "rms", "ve2", "rstd2"))
        mhalf, eps5, eps6 = (sb(n, [P, NT]) for n in ("mhalf", "eps5", "eps6"))
        hn_h, hn_l = sb("hn_h", [P, L], F16), sb("hn_l", [P, L], F16)
        vp = sb("vp", [P, ML, L + 2 * PADL])
        z_h, z_l = sb("z_h", [P, L], F16), sb("z_l", [P, L], F16)
        cv = sb("cv", [P, ML, L])
        sbv = sb("sbv", [P, ML, L])
        s_h, s_l = over_mat([ML, L], F16), sb("s_l", [P, ML, L], F16)
        gate = sb("gate", [P, ML, L])
        gy = cv
        g_h, g_l = sb("g_h", [P, ML, L], F16), sb("g_l", [P, ML, L], F16)
        h2_h, h2_l = sb("h2_h", [P, L], F16), sb("h2_l", [P, L], F16)
        nx_h, nx_l = hn_h, hn_l

        def routes(t):
            return t[:].rearrange("p m l -> p (m l)")[:, 0:NT * E].rearrange("p (n e) -> p n e", n=NT)

        lg, pr, rp = routes(gate), routes(sbv), routes(cv)
        cw = lg
        mx = sb("mx", [P, NT, TOPK])
        sm, sme, rs = sb("sm", [P, NT]), sb("sme", [P, NT]), sb("rs", [P, NT])
        cT0, cT1 = (t.rearrange("p n d -> p (n d)") for t in (hb, h2))
        ss = sb("ss", [INTER, L])
        ss_h, ss_l = sb("ss_h", [INTER, L], F16), sb("ss_l", [INTER, L], F16)
        ring = sb("ring", [P, 2 * URING, L])
        su, gw = ring[:, 0:URING], ring[:, URING:]
        gw_h, gw_l = sb("gw_h", [P, BODY, L], F16), sb("gw_l", [P, BODY, L], F16)
        accs = t1.rearrange("p n d -> p (n d)")
        sq = hn
        stage_sb = ring[:, 0:4].rearrange("p (a b) l -> p a (b l)", a=2)
        gmag, gsgn = (t[:].rearrange("p m (u j d) -> p (m u) j d", u=2, j=2) for t in (cv, sbv))
        scb = gate[:, 0, :].rearrange("p (b r) -> p b r", b=B)
        wf = cbr[:, 0, 0:640]
        gmat, qmat = cbr[:, 1, 0:P], cbr[:, 1, P:P + DI]
        ak, a1, bm4 = (cbr[:, 2, i * DI:(i + 1) * DI].rearrange("p (m k) -> p m k", m=ML) for i in range(3))

        s = {n: sem(n) for n in (
            "ld_idf ld_vec ld_mat ld_rows ld_sd x_loaded out_stored out_free ot_set cT_stored "
            "pads mhalf_set ak_set silu_c scb_set mod_ps mod_half mod_set gmag_set gsgn_set gates_set "
            "fold1 fold1_sb fold2 fold3 win_f win_hi win_lo wz_f wz_hi wz_lo wab_f wab_hi wab_lo wo_f wo_hi wo_lo jb_set bz_set by_set "
            "piece_scaled piece_hi piece_lo "
            "stats aggr ve_set rstd_set t1_set h_set sq_set mse_set rms_set hn_set hnT hnT_hi hnT_lo "
            "val_ps z_ps gate_ps v_sb z_hi z_lo conv0 conv1 gate_sb silu_b s_hi s_lo y_ps gy_set g_hi g_lo o_ps "
            "hb_set hg_set base_set t2_set x2_set stats2 aggr2 ve2_set rstd2_set xc2_set h2_set h2T h2T_hi h2T_lo "
            "lg_ps lg_set pr_set mx_set rp_set cw_set sm_set sme_set rs_set cn_set cT cT_sb handed xf_set "
            "sh_up sh_silu sh_hi sh_lo up_ready silu_done gw_done hi_act hi_dve lo_pool lo_dve acc_ready acc_sb accT t3_set"
        ).split()}
        cb_landed = [sem(f"cb_landed{i}") for i in range(CSLOTS)]
        ld_piece = [sem("ld_piece0"), sem("ld_piece1")]

        wpiece = [wg[:, i * PIECE * P:(i + 1) * PIECE * P] for i in range(NPIECE)] + \
                 [wd[:, i * PIECE * P:(i + 1) * PIECE * P] for i in range(NPIECE)]
        xv = x.rearrange("b (n p) d -> b p n d", p=P)
        ov = out.rearrange("b (n p) d -> b p n d", p=P)

        def bc(ap, n):
            return ap.rearrange("p (t o) -> p t o", o=1).broadcast_to([P, NT, n])

        def modr(c, j, k=NT):
            return mod[:, bass.ds(c, 1), j * D:(j + 1) * D].broadcast_to([P, k, D])

        def cached_wait(eng, sem_, c):
            eng.wait_ge(s["ld_vec"], 16)
            eng.wait_ge(sem_, c + 1)

        def hi_wait(eng, c, i8, k):
            eng.wait_ge(s["hi_dve" if k % 2 else "hi_act"], c * (BLOCKS // 2) + i8 * (BODY // 2) + (k // 2 + 1))

        def lo_wait(eng, c, i8, k):
            if k == BODY - 1:
                eng.wait_ge(s["lo_dve"], c * (BLOCKS // BODY) + i8 + 1)
            else:
                eng.wait_ge(s["lo_pool"], c * (BLOCKS // BODY * (BODY - 1)) + i8 * (BODY - 1) + (k + 1))

        def before(i8, k, n):
            return (i8, k - n) if k >= n else (i8 - 1, k - n + BODY)

        def count(c, i8, k):
            return c * BLOCKS + i8 * BODY + (k + 1)

        def chunks(eng, prologue, block, stage, end):
            prologue()
            with eng.Fori(0, B - 1) as c:
                for g in range(GROUPS):
                    for k in range(4):
                        block(c, g // 2, g % 2 * 4 + k, g < 2)
                    stage(c + 1, g)
                end(c)
            for k in range(BODY):
                block(B - 1, 0, k, True)
            with eng.Fori(1, BLOCKS // BODY) as i8:
                for k in range(BODY):
                    block(B - 1, i8, k, False)
            end(B - 1)

        block = ctx.enter_context(nc.Block())

        @block.sync
        def _(sp):
            sp.dma_start(vec[:], vecs).then_inc(s["ld_vec"], 16)
            sp.dma_start(xt[:], xv[0]).then_inc(s["x_loaded"], 16)
            sp.dma_start(mat[:], mats).then_inc(s["ld_mat"], 16)
            sp.dma_start(sdf[:], sdT).then_inc(s["ld_sd"], 16)
            sp.dma_start(brow[:], rows.broadcast_to([P, E + D])).then_inc(s["ld_rows"], 16)
            sp.dma_start(idf[:], idf_c).then_inc(s["ld_idf"], 16)
            for i in range(2 * NPIECE):
                if i >= 2:
                    sp.wait_ge(s["piece_lo"], i - 1)
                sp.dma_start(stage_sb[:, i % 2, :], wpiece[i]).then_inc(ld_piece[i % 2], 16)
            sp.sem_inc(s["out_free"], 1)

            def load_cb(c, j4, q):
                row = c_dram[bass.ds(c, 1)].rearrange("a (g h w) t -> a g h (w t)", h=2, w=4)
                g = j4 * 2 + q // 2
                src = row[:, bass.ds(g, 1), :, q % 2 * SLOTB * L:(q % 2 + 1) * SLOTB * L]\
                    .rearrange("a g h t -> (a g) h t").broadcast_to([INTER, 2, SLOTB * L])
                sp.dma_start(cbr[:, q, :], src).then_inc(cb_landed[q], 16)

            def body_cb(c, j4):
                for q in range(CSLOTS):
                    sp.wait_ge(s["gw_done"], count(c, j4 - 1, 2 * q + 1))
                    load_cb(c, j4, q)

            def store(c):
                sp.wait_ge(s["ot_set"], c + 1)
                sp.dma_start(ov[bass.ds(c, 1)].rearrange("a p n d -> (a p) n d"), ot[:]).then_inc(s["out_stored"], 16)

            sp.wait_ge(s["cT_stored"], 32)
            for q in range(CSLOTS):
                load_cb(0, 0, q)
            with sp.Fori(1, BLOCKS // BODY) as j4:
                body_cb(0, j4)
            with sp.Fori(1, B) as c:
                sp.wait_ge(s["cT_stored"], c * 32 + 32)
                for q in range(CSLOTS):
                    sp.wait_ge(s["gw_done"], count(c - 1, BLOCKS // BODY - 1, 2 * q + 1))
                    load_cb(c, 0, q)
                store(c - 1)
                with sp.Fori(1, BLOCKS // BODY) as j4:
                    body_cb(c, j4)
                sp.wait_ge(s["out_stored"], c * 16)
                sp.sem_inc(s["out_free"], 1)
            store(B - 1)
            sp.wait_ge(s["out_stored"], 16 * B)

        @block.gpsimd
        def _(pool):
            g = nc.gpsimd
            for t, value in ((mhalf, -0.5), (eps5, 1e-5), (eps6, 1e-6)):
                g.memset(t[:], value).then_inc(s["mhalf_set"], 1)
            pool.wait_ge(s["mhalf_set"], 3)
            for t in (ak, a1, bm4, vp[:], z_h[:], z_l[:]):
                g.memset(t, 0.0).then_inc(s["pads"], 1)
            pool.wait_ge(s["mod_set"], 2 * B)
            gates = mod[:].rearrange("p b (k j d) -> p b k j d", k=2, j=3)[:, :, :, 2, :]
            pool.wait_ge(s["gmag_set"], 1)
            g.tensor_scalar(gsgn[:], gates, 0.0, None, ALU.is_ge).then_inc(s["gsgn_set"], 1)
            pool.wait_ge(s["gsgn_set"], 1)
            g.tensor_scalar(gsgn[:], gsgn[:], 2.0, -1.0, ALU.mult, ALU.add).then_inc(s["gsgn_set"], 1)
            pool.wait_ge(s["gsgn_set"], 2)
            g.tensor_scalar(gmag[:], gmag[:], 0.25, None, ALU.max).then_inc(s["gsgn_set"], 1)
            pool.wait_ge(s["gsgn_set"], 3)
            g.tensor_tensor(gates, gsgn[:], gmag[:], ALU.mult).then_inc(s["gates_set"], 1)
            pool.wait_ge(s["gates_set"], 1)

            def stage(c, n):
                if n == 0:
                    pool.wait_ge(s["aggr"], c + 1)
                    g.tensor_tensor(ve[:], mv[:, :, 1], eps5[:], ALU.add).then_inc(s["ve_set"], 1)
                    pool.wait_ge(s["ve_set"], c + 1)
                    g.tensor_tensor(rstd[:], ve[:], mhalf[:], ALU.pow).then_inc(s["rstd_set"], 1)
                elif n == 1:
                    pool.wait_ge(s["sq_set"], c + 1)
                    g.tensor_tensor(mse[:], ms[:], eps6[:], ALU.add).then_inc(s["mse_set"], 1)
                    pool.wait_ge(s["mse_set"], c + 1)
                    g.tensor_tensor(rms[:], mse[:], mhalf[:], ALU.pow).then_inc(s["rms_set"], 1)
                elif n == 2:
                    g.tensor_tensor(hb[:], h[:], outb.rearrange("p (o d) -> p o d", o=1).broadcast_to([P, NT, D]),
                                    ALU.add).then_inc(s["hb_set"], 1)
                elif n == 4:
                    pool.wait_ge(s["hb_set"], c + 1)
                    g.tensor_tensor(hb[:], hb[:], modr(c, 2), ALU.mult).then_inc(s["hg_set"], 1)
                elif n == 6:
                    pool.wait_ge(s["hg_set"], c + 1)
                    g.tensor_tensor(base[:], hb[:], xt[:], ALU.add).then_inc(s["base_set"], 1)
                elif n == 14:
                    pool.wait_ge(s["aggr2"], c + 1)
                    g.tensor_tensor(ve2[:], mv2[:, :, 1], eps5[:], ALU.add).then_inc(s["ve2_set"], 1)
                    pool.wait_ge(s["ve2_set"], c + 1)
                    g.tensor_tensor(rstd2[:], ve2[:], mhalf[:], ALU.pow).then_inc(s["rstd2_set"], 1)

            def low(c, i8, k, first):
                if k == BODY - 1:
                    return
                hi_wait(pool, c, i8, k)
                g.tensor_tensor(gw_l[:, k, :], gw[:, k % URING, :], gw_h[:, k, :], ALU.subtract)\
                    .then_inc(s["lo_pool"], 1)

            chunks(pool, lambda: [stage(0, n) for n in range(GROUPS)], low, stage, lambda c: None)

        @block.scalar
        def _(act):
            a = nc.scalar.activation
            act.wait_ge(s["ld_vec"], 16)
            a(sct[:], v("cT", 0, B), ACT.Silu).then_inc(s["silu_c"], 1)
            act.wait_ge(s["win_f"], 1)
            a(win_h[:], wf[:, 0:2 * DI], ACT.Copy).then_inc(s["win_hi"], 1)
            for b in range(B):
                act.wait_ge(s["mod_ps"], 2 * b + 1)
                a(mod[:, b, 0:512], pa[:], ACT.Copy).then_inc(s["mod_half"], 1)
                act.wait_ge(s["mod_ps"], 2 * b + 2)
                a(mod[:, b, 512:768], pb[:, 0:256], ACT.Copy).then_inc(s["mod_half"], 1)
            act.wait_ge(s["mod_set"], 2 * B)
            a(gmag[:], mod[:].rearrange("p b (k j d) -> p b k j d", k=2, j=3)[:, :, :, 2, :], ACT.Abs)\
                .then_inc(s["gmag_set"], 1)
            act.wait_ge(s["wz_f"], 1)
            a(wz_h[:], wf[:, 512:640], ACT.Copy).then_inc(s["wz_hi"], 1)
            act.wait_ge(s["ld_mat"], 16)
            a(wo_h[:].rearrange("p m d -> p (m d)"), m("outT"), ACT.Copy, scale=WS).then_inc(s["wo_hi"], 1)
            a(wr_h[:], m("rT"), ACT.Copy, scale=ES_SCALE).then_inc(s["wo_hi"], 1)
            a(sg_h[:], m("sgT"), ACT.Copy, scale=ES_SCALE).then_inc(s["wo_hi"], 1)
            act.wait_ge(s["ld_sd"], 16)
            a(sd_h[:], sdf[:], ACT.Copy, scale=ES_SCALE).then_inc(s["wo_hi"], 1)
            act.wait_ge(s["fold3"], 1)
            a(wa_h[:], pa[:, 0:DI], ACT.Copy).then_inc(s["wab_hi"], 1)
            act.wait_ge(s["fold3"], 2)
            a(wb_h[:].rearrange("p m o -> p (m o)"), pb[:], ACT.Copy, scale=WS).then_inc(s["wab_hi"], 1)
            def piece(i):
                dst = (wg_h if i < NPIECE else wd_h)[:, i % NPIECE * PIECE * P:(i % NPIECE + 1) * PIECE * P]
                act.wait_ge(ld_piece[i % 2], 16 * (i // 2 + 1))
                a(dst, stage_sb[:, i % 2, :], ACT.Copy, scale=ES_SCALE).then_inc(s["piece_hi"], 1)

            def stage(c, n):
                if n == 1:
                    for t in range(NT):
                        act.wait_ge(s["h_set"], c * NT + t + 1)
                        last = a(sq[:, t, :], h[:, t, :], ACT.Square, scale=D ** -0.5, accum_out=ms[:, t:t + 1])
                    last.then_inc(s["sq_set"], 1)
                elif n == 3:
                    act.wait_ge(s["hnT"], c + 1)
                    a(hn_h[:], pa[:], ACT.Copy).then_inc(s["hnT_hi"], 1)
                elif n == 4:
                    for k in range(ML):
                        act.wait_ge(s["val_ps"], c * ML + k + 1)
                        a(vp[:, k, PADL:PADL + L], (pb, pc)[k][:], ACT.Identity, bias=v("in_b", ML + k),
                          scale=1.0 / WS).then_inc(s["v_sb"], 1)
                elif n == 5:
                    act.wait_ge(s["z_ps"], c + 1)
                    for k in range(DC):
                        lo, hi = max(0, 1 - k), min(L, L + 1 - k)
                        q = slice(32 * k, 32 * k + 32)
                        a(z_h[q, lo:hi], pa[q, lo + k - 1:hi + k - 1], ACT.Identity, bias=bz[q, 0:1])\
                            .then_inc(s["z_hi"], 1)
                elif n in (6, 7):
                    k = n - 6
                    act.wait_ge(s["gate_ps"], c * ML + k + 1)
                    a(gate[:, k, :], (pb, pc)[k][:], ACT.Sigmoid, bias=v("in_b", k), scale=1.0 / WS)\
                        .then_inc(s["gate_sb"], 1)
                elif n == 10:
                    for k in range(ML):
                        act.wait_ge(s[f"conv{k}"], c * KS + KS)
                        a(sbv[:, k, :], cv[:, k, :], ACT.Silu).then_inc(s["silu_b"], 1)
                elif n == 16:
                    act.wait_ge(s["h2T"], c + 1)
                    a(nx_h[:], pa[:], ACT.Copy).then_inc(s["h2T_hi"], 1)
                elif n == 17:
                    act.wait_ge(s["lg_set"], c * 2 + 2)
                    a(pr[:], lg[:], ACT.Sigmoid).then_inc(s["pr_set"], 1)
                    act.wait_ge(s["sh_up"], c + 1)
                    a(ss[:], pa[0:INTER, :], ACT.Silu, scale=1.0 / ES_SCALE).then_inc(s["sh_silu"], 1)
                elif n == 18:
                    act.wait_ge(s["sh_silu"], c + 1)
                    a(ss_h[:], ss[:], ACT.Copy).then_inc(s["sh_hi"], 1)
                elif n == 19:
                    act.wait_ge(s["cT"], c + 1)
                    a(cT0, pb[:], ACT.Copy).then_inc(s["cT_sb"], 1)
                    a(cT1[0:E - P, :], pc[0:E - P, :], ACT.Copy).then_inc(s["cT_sb"], 1)
                    act.wait_ge(s["cT_sb"], c * 2 + 2)
                    dst = c_dram[bass.ds(c, 1)].rearrange("a e t -> (a e) t")
                    act.dma_start(dst[0:P, :], cT0).then_inc(s["cT_stored"], 16)
                    act.dma_start(dst[P:E, :], cT1[0:E - P, :]).then_inc(s["cT_stored"], 16)

            def hidden(c, i8, k, first):
                act.wait_ge(s["up_ready"], count(c, i8, k))
                if not first or k >= URING:
                    act.wait_ge(s["gw_done"], count(c, i8, k - URING))
                a(su[:, k % URING, :], up_ps[k % URING][:], ACT.Silu, scale=1.0 / ES_SCALE)\
                    .then_inc(s["silu_done"], 1)
                if k % 2:
                    act.wait_ge(s["gw_done"], count(c, i8, k - 1))
                    a(gw_h[:, k - 1, :], gw[:, (k - 1) % URING, :], ACT.Copy).then_inc(s["hi_act"], 1)
                if first and k == 0 and not isinstance(c, int):
                    act.wait_ge(s["x2_set"], c + 1)
                    act.dma_start(xt[:], xv[bass.ds(c + 1, 1)].rearrange("a p n d -> (a p) n d"))\
                        .then_inc(s["x_loaded"], 16)

            def prologue():
                for n in range(GROUPS):
                    stage(0, n)
                    if n < 2 * NPIECE:
                        piece(n)

            def end(c):
                act.wait_ge(s["acc_ready"], c + 1)
                a(accs, acc_ps[:], ACT.Copy, scale=1.0 / ES_SCALE).then_inc(s["acc_sb"], 1)

            chunks(act, prologue, hidden, stage, end)

        @block.vector
        def _(dve):
            e = nc.vector
            dve.wait_ge(s["ld_vec"], 16)
            dve.wait_ge(s["pads"], 6)
            for mm in range(ML):
                for k in range(DC):
                    e.tensor_scalar(ak[:, mm, 32 * k:32 * k + DS], v("A", mm * DS, DS), v("dwa_k", mm * DC + k), None,
                                    ALU.mult).then_inc(s["ak_set"], 1)
                    e.tensor_copy(bm4[:, mm, 32 * k:32 * k + DS], v("BmT", mm * DS, DS)).then_inc(s["ak_set"], 1)
                e.tensor_copy(a1[:, mm, 32:32 + DS], v("A", mm * DS, DS)).then_inc(s["ak_set"], 1)
            dve.wait_ge(s["silu_c"], 1)
            e.tensor_copy(scb[:], sct[:].rearrange("p (b o) -> p b o", o=1).broadcast_to([P, B, P]))\
                .then_inc(s["scb_set"], 1)
            dve.wait_ge(s["ld_mat"], 16)
            e.tensor_scalar(wf[:, 0:2 * DI], m("in_wT"), v("norm_w"), WS, ALU.mult, ALU.mult).then_inc(s["win_f"], 1)
            dve.wait_ge(s["win_hi"], 1)
            e.tensor_tensor(win_l[:], wf[:, 0:2 * DI], win_h[:], ALU.subtract).then_inc(s["win_lo"], 1)
            for b in range(B):
                for j in (1, 4):
                    dve.wait_ge(s["mod_half"], 2 * b + (2 if j == 4 else 1))
                    r = mod[:, b, j * D:(j + 1) * D]
                    e.tensor_scalar(r, r, 1.0, None, ALU.add).then_inc(s["mod_set"], 1)
            dve.wait_ge(s["fold1"], 1)
            e.tensor_copy(gmat[:], pc[:, 0:P]).then_inc(s["fold1_sb"], 1)
            e.tensor_copy(qmat[:], pc[:, P:P + DI]).then_inc(s["fold1_sb"], 1)
            e.tensor_tensor(jb[:], pc[:, 384:385], v("hb_b"), ALU.add).then_inc(s["jb_set"], 1)
            dve.wait_ge(s["fold2"], 1)
            e.tensor_scalar(wf[:, 512:640], acc_ps[:, 0:P], v("norm_w"), WS, ALU.mult, ALU.mult)\
                .then_inc(s["wz_f"], 1)
            e.tensor_scalar(bz[:], acc_ps[:, 128:129], WS, None, ALU.mult).then_inc(s["bz_set"], 1)
            dve.wait_ge(s["wz_hi"], 1)
            e.tensor_tensor(wz_l[:], wf[:, 512:640], wz_h[:], ALU.subtract).then_inc(s["wz_lo"], 1)
            for i, (hi, src, lo) in enumerate(((wo_h[:].rearrange("p m d -> p (m d)"), m("outT"),
                                                wo_l[:].rearrange("p m d -> p (m d)")),
                                               (wr_h[:], m("rT"), wr_l[:]), (sg_h[:], m("sgT"), sg_l[:]),
                                               (sd_h[:], sdf[:], sd_l[:]))):
                dve.wait_ge(s["wo_hi"], i + 1)
                e.scalar_tensor_tensor(out=lo, in0=src, scalar=WS if i == 0 else ES_SCALE, in1=hi, op0=ALU.mult,
                                       op1=ALU.subtract).then_inc(s["wo_lo"], 1)
            dve.wait_ge(s["wab_hi"], 1)
            e.tensor_tensor(wa_l[:], pa[:, 0:DI], wa_h[:], ALU.subtract).then_inc(s["wab_lo"], 1)
            dve.wait_ge(s["wab_hi"], 2)
            e.scalar_tensor_tensor(out=wb_l[:].rearrange("p m o -> p (m o)"), in0=pb[:], scalar=WS,
                                   in1=wb_h[:].rearrange("p m o -> p (m o)"), op0=ALU.mult,
                                   op1=ALU.subtract).then_inc(s["wab_lo"], 1)
            e.tensor_tensor(by[:], pa[:, 256:256 + ML], v("fuse_b", 0, ML), ALU.add).then_inc(s["by_set"], 1)
            dve.wait_ge(s["by_set"], 1)
            e.tensor_scalar(by[:], by[:], WS, None, ALU.mult).then_inc(s["by_set"], 1)
            dve.wait_ge(s["by_set"], 2)
            dve.wait_ge(s["gates_set"], 1)
            dve.wait_ge(s["ld_rows"], 16)

            def piece(i):
                at = slice(i % NPIECE * PIECE * P, (i % NPIECE + 1) * PIECE * P)
                hi, lo = ((wg_h, wg_l) if i < NPIECE else (wd_h, wd_l))
                dve.wait_ge(s["piece_hi"], i + 1)
                e.scalar_tensor_tensor(out=lo[:, at], in0=stage_sb[:, i % 2, :], scalar=ES_SCALE, in1=hi[:, at],
                                       op0=ALU.mult, op1=ALU.subtract).then_inc(s["piece_lo"], 1)

            def row(c, j):
                return mod[:, bass.ds(c, 1), j * D:(j + 1) * D].rearrange("p a d -> p (a d)")

            def conv(c, k):
                for mm in range(ML):
                    src = vp[:, mm, k:k + L]
                    if k == 0:
                        dve.wait_ge(s["v_sb"], c * ML + mm + 1)
                        e.tensor_scalar(cv[:, mm, :], src, v("sym_k", mm * KS), v("sym_b", mm), ALU.mult,
                                        ALU.add).then_inc(s[f"conv{mm}"], 1)
                    else:
                        dve.wait_ge(s[f"conv{mm}"], c * KS + k)
                        e.scalar_tensor_tensor(out=cv[:, mm, :], in0=src, scalar=v("sym_k", mm * KS + k),
                                               in1=cv[:, mm, :], op0=ALU.mult, op1=ALU.add)\
                            .then_inc(s[f"conv{mm}"], 1)

            def stage(c, n):
                if n == 0:
                    dve.wait_ge(s["x_loaded"], c * 16 + 16)
                    dve.wait_ge(s["mod_set"], c + 1)
                    for t in range(NT):
                        last = e.bn_stats(st[:, t, :], xt[:, t, :])
                    last.then_inc(s["stats"], 1)
                    cached_wait(dve, s["stats"], c)
                    for t in range(NT):
                        last = e.bn_aggr(mv[:, t, :], st[:, t, :])
                    last.then_inc(s["aggr"], 1)
                    dve.wait_ge(s["aggr"], c + 1)
                    for t in range(NT):
                        e.scalar_tensor_tensor(out=t1[:, t, :], in0=xt[:, t, :], scalar=mv[:, t, 0:1], in1=row(c, 1),
                                               op0=ALU.subtract, op1=ALU.mult).then_inc(s["t1_set"], 1)
                elif n == 1:
                    dve.wait_ge(s["rstd_set"], c + 1)
                    for t in range(NT):
                        dve.wait_ge(s["t1_set"], c * NT + t + 1)
                        e.scalar_tensor_tensor(out=h[:, t, :], in0=t1[:, t, :], scalar=rstd[:, t:t + 1],
                                               in1=row(c, 0), op0=ALU.mult, op1=ALU.add).then_inc(s["h_set"], 1)
                elif n == 2:
                    dve.wait_ge(s["rms_set"], c + 1)
                    e.tensor_tensor(hn[:], h[:], bc(rms[:], D), ALU.mult).then_inc(s["hn_set"], 1)
                elif n == 3:
                    dve.wait_ge(s["hnT_hi"], c + 1)
                    e.tensor_tensor(hn_l[:], pa[:], hn_h[:], ALU.subtract).then_inc(s["hnT_lo"], 1)
                elif n == 5:
                    conv(c, 0)
                    for k in range(DC):
                        lo, hi = max(0, 1 - k), min(L, L + 1 - k)
                        q = slice(32 * k, 32 * k + 32)
                        dve.wait_ge(s["z_hi"], c * DC + k + 1)
                        e.scalar_tensor_tensor(out=z_l[q, lo:hi], in0=pa[q, lo + k - 1:hi + k - 1],
                                               scalar=bz[q, 0:1], in1=z_h[q, lo:hi], op0=ALU.add,
                                               op1=ALU.subtract).then_inc(s["z_lo"], 1)
                elif n in (6, 7, 8, 9):
                    conv(c, 2 * n - 11)
                    conv(c, 2 * n - 10)
                elif n == 10:
                    dve.wait_ge(s["silu_b"], c * ML + ML)
                    e.tensor_copy(s_h, sbv[:]).then_inc(s["s_hi"], 1)
                    dve.wait_ge(s["s_hi"], c + 1)
                    e.tensor_tensor(s_l[:], sbv[:], s_h, ALU.subtract).then_inc(s["s_lo"], 1)
                elif n == 11:
                    dve.wait_ge(s["gate_sb"], c * ML + ML)
                    for k in range(ML):
                        dve.wait_ge(s["y_ps"], c * ML + k + 1)
                        e.scalar_tensor_tensor(out=gy[:, k, :], in0=(pb, pc)[k][:], scalar=by[:, k:k + 1],
                                               in1=gate[:, k, :], op0=ALU.add, op1=ALU.mult).then_inc(s["gy_set"], 1)
                elif n == 12:
                    dve.wait_ge(s["gy_set"], c * ML + ML)
                    e.tensor_copy(g_h[:], gy[:]).then_inc(s["g_hi"], 1)
                    dve.wait_ge(s["g_hi"], c + 1)
                    e.tensor_tensor(g_l[:], gy[:], g_h[:], ALU.subtract).then_inc(s["g_lo"], 1)
                elif n == 13:
                    dve.wait_ge(s["o_ps"], c + 1)
                    e.scalar_tensor_tensor(out=t2[:], in0=pa[:].rearrange("p (n d) -> p n d", d=D),
                                           scalar=1.0 / (WS * WS), in1=modr(c, 2), op0=ALU.mult, op1=ALU.mult)\
                        .then_inc(s["t2_set"], 1)
                    if not isinstance(c, int):
                        dve.wait_ge(s["xf_set"], c)
                    dve.wait_ge(s["base_set"], c + 1)
                    dve.wait_ge(s["t2_set"], c + 1)
                    e.tensor_tensor(x2[:], t2[:], base[:], ALU.add).then_inc(s["x2_set"], 1)
                    dve.wait_ge(s["x2_set"], c + 1)
                    for t in range(NT):
                        last = e.bn_stats(st2[:, t, :], x2[:, t, :])
                    last.then_inc(s["stats2"], 1)
                elif n == 14:
                    cached_wait(dve, s["stats2"], c)
                    for t in range(NT):
                        last = e.bn_aggr(mv2[:, t, :], st2[:, t, :])
                    last.then_inc(s["aggr2"], 1)
                    dve.wait_ge(s["aggr2"], c + 1)
                    for t in range(NT):
                        e.scalar_tensor_tensor(out=xc2[:, t, :], in0=x2[:, t, :], scalar=mv2[:, t, 0:1],
                                               in1=row(c, 4), op0=ALU.subtract, op1=ALU.mult)\
                            .then_inc(s["xc2_set"], 1)
                elif n == 15:
                    dve.wait_ge(s["rstd2_set"], c + 1)
                    for t in range(NT):
                        dve.wait_ge(s["xc2_set"], c * NT + t + 1)
                        e.scalar_tensor_tensor(out=h2[:, t, :], in0=xc2[:, t, :], scalar=rstd2[:, t:t + 1],
                                               in1=row(c, 3), op0=ALU.mult, op1=ALU.add).then_inc(s["h2_set"], 1)
                elif n == 16:
                    dve.wait_ge(s["h2T_hi"], c + 1)
                    e.tensor_tensor(nx_l[:], pa[:], nx_h[:], ALU.subtract).then_inc(s["h2T_lo"], 1)
                    for k in range(2):
                        dve.wait_ge(s["lg_ps"], c * 2 + k + 1)
                        e.scalar_tensor_tensor(
                            out=lg[:, 2 * k:2 * k + 2, :],
                            in0=(pb, pc)[k][:, 0:2 * E].rearrange("p (n e) -> p n e", n=2), scalar=1.0 / ES_SCALE,
                            in1=ebias.rearrange("p (o e) -> p o e", o=1).broadcast_to([P, 2, E]), op0=ALU.mult,
                            op1=ALU.add).then_inc(s["lg_set"], 1)
                elif n == 17:
                    cached_wait(dve, s["pr_set"], c)
                    for t in range(NT):
                        last = e.max(mx[:, t, :], pr[:, t, :])
                    last.then_inc(s["mx_set"], 1)
                    cached_wait(dve, s["mx_set"], c)
                    for t in range(NT):
                        last = e.match_replace(rp[:, t, :], mx[:, t, :], pr[:, t, :], 0.0)
                    last.then_inc(s["rp_set"], 1)
                elif n == 18:
                    e.tensor_reduce(sm[:], mx[:], AX.X, ALU.add).then_inc(s["sm_set"], 1)
                    dve.wait_ge(s["rp_set"], c + 1)
                    e.tensor_tensor(cw, pr, rp, ALU.subtract).then_inc(s["cw_set"], 1)
                    dve.wait_ge(s["sm_set"], c + 1)
                    e.tensor_scalar(sme[:], sm[:], 1e-9, 1.0 / ROUTED_SCALE, ALU.add, ALU.mult)\
                        .then_inc(s["sme_set"], 1)
                    dve.wait_ge(s["sme_set"], c + 1)
                    e.reciprocal(rs[:], sme[:]).then_inc(s["rs_set"], 1)
                    dve.wait_ge(s["rs_set"], c + 1)
                    dve.wait_ge(s["cw_set"], c + 1)
                    e.tensor_tensor(cw, cw, bc(rs[:], E), ALU.mult).then_inc(s["cn_set"], 1)
                    dve.wait_ge(s["sh_hi"], c + 1)
                    e.tensor_tensor(ss_l[:], ss[:], ss_h[:], ALU.subtract).then_inc(s["sh_lo"], 1)

            def high(c, i8, k):
                dve.wait_ge(s["gw_done"], count(c, i8, k))
                e.tensor_copy(gw_h[:, k, :], gw[:, k % URING, :]).then_inc(s["hi_dve"], 1)

            def low(c, i8, k):
                hi_wait(dve, c, i8, k)
                e.tensor_tensor(gw_l[:, k, :], gw[:, k % URING, :], gw_h[:, k, :], ALU.subtract)\
                    .then_inc(s["lo_dve"], 1)

            def weigh(c, i8, k, first):
                dve.wait_ge(s["silu_done"], count(c, i8, k))
                dve.wait_ge(cb_landed[k // 2], c * (16 * LOADS // CSLOTS) + i8 * 16 + 16)
                if not first or k >= URING:
                    lo_wait(dve, c, *before(i8, k, URING))
                e.tensor_tensor(gw[:, k % URING, :], su[:, k % URING, :],
                                cbr[:, k // 2, k % 2 * L:(k % 2 + 1) * L], ALU.mult).then_inc(s["gw_done"], 1)
                if k % 2 == 0 and not (first and k == 0):
                    high(c, *before(i8, k, 1))
                if k == 1 and not first:
                    low(c, i8 - 1, BODY - 1)

            def hand(c):
                e.tensor_copy(h2_h[:], nx_h[:]).then_inc(s["handed"], 1)
                e.tensor_copy(h2_l[:], nx_l[:]).then_inc(s["handed"], 1)

            def prologue():
                for n in range(GROUPS):
                    stage(0, n)
                    if n < 2 * NPIECE:
                        piece(n)
                hand(0)
                e.tensor_copy(xf[:], x2[:]).then_inc(s["xf_set"], 1)

            def end(c):
                high(c, BLOCKS // BODY - 1, BODY - 1)
                low(c, BLOCKS // BODY - 1, BODY - 1)
                if not isinstance(c, int):
                    dve.wait_ge(s["up_ready"], c * BLOCKS + BLOCKS)
                    hand(c + 1)
                dve.wait_ge(s["accT"], c + 1)
                e.tensor_tensor(t3[:], pa[:].rearrange("p (n d) -> p n d", d=D), modr(c, 5), ALU.mult)\
                    .then_inc(s["t3_set"], 1)
                dve.wait_ge(s["out_free"], c + 1)
                dve.wait_ge(s["t3_set"], c + 1)
                e.tensor_tensor(ot[:], t3[:], xf[:], ALU.add).then_inc(s["ot_set"], 1)
                if not isinstance(c, int):
                    dve.wait_ge(s["ot_set"], c + 1)
                    e.tensor_copy(xf[:], x2[:]).then_inc(s["xf_set"], 1)

            chunks(dve, prologue, weigh, stage, end)

        @block.tensor
        def _(pe):
            mm = nc.tensor.matmul

            def split(dst, lhs, rhs, start=True, stop=True):
                (lh, ll), (rh, rl) = lhs, rhs
                mm(dst, lh, rh, start=start, stop=False)
                mm(dst, ll, rh, start=False, stop=False)
                return mm(dst, lh, rl, start=False, stop=stop)

            pe.wait_ge(s["ld_mat"], 16)
            pe.wait_ge(s["scb_set"], 1)
            for b in range(B):
                if b:
                    pe.wait_ge(s["mod_half"], 2 * b)
                mm(pa[:], scb[:, b, :], m("wmod", 0, 512)).then_inc(s["mod_ps"], 1)
                mm(pb[:, 0:256], scb[:, b, :], m("wmod", 512, 256)).then_inc(s["mod_ps"], 1)
            pe.wait_ge(s["ak_set"], ML * (2 * DC + 1))
            for k in range(ML):
                mm(pc[:, 0:P], m("haT", k * P, P), bm4[:, k, :], start=(k == 0), stop=(k == ML - 1))
            for k in range(ML):
                mm(pc[:, P:P + DI], m("hbT", k * P, P), m("pw", k * DI, DI), start=(k == 0), stop=(k == ML - 1))
            for k in range(ML):
                last = mm(pc[:, 384:385], m("hbT", k * P, P), v("pw_b", k), start=(k == 0), stop=(k == ML - 1))
            last.then_inc(s["fold1"], 1)
            for k in range(ML):
                mm(acc_ps[:, 0:P], m("inv", k * D, D), ak[:, k, :], start=(k == 0), stop=(k == ML - 1))
            for k in range(ML):
                mm(acc_ps[:, 128:129], ak[:, k, :], v("in_b", ML + k), start=(k == 0), stop=False)
            for k in range(ML):
                last = mm(acc_ps[:, 128:129], a1[:, k, :], v("dwa_b", k), start=False, stop=(k == ML - 1))
            last.then_inc(s["fold2"], 1)
            pe.wait_ge(s["fold1_sb"], 2)
            pe.wait_ge(s["jb_set"], 1)
            pe.wait_ge(s["mod_half"], 2 * B)
            mm(pa[:, 0:DI], gmat[:], m("fuseT", 0, DI))
            for k in range(ML):
                mm(pa[:, 256 + k:257 + k], m("fuseT", k * P, P), v("ha_b"), start=True, stop=False)
                last = mm(pa[:, 256 + k:257 + k], m("fuseT", DI + k * P, P), jb[:], start=False, stop=True)
            last.then_inc(s["fold3"], 1)
            for k in range(ML):
                last = mm(pb[:, k * DI:(k + 1) * DI], qmat[:, k * P:(k + 1) * P], m("fuseT", DI, DI))
            last.then_inc(s["fold3"], 1)
            pe.wait_ge(s["win_lo"], 1)
            pe.wait_ge(s["wz_lo"], 1)
            pe.wait_ge(s["wo_lo"], 4)
            pe.wait_ge(s["wab_lo"], 2)
            pe.wait_ge(s["by_set"], 1)
            pe.wait_ge(s["ld_idf"], 16)

            hnT = (hn_h[:], hn_l[:])
            nxT = (nx_h[:], nx_l[:])
            h2T = (h2_h[:], h2_l[:])

            def stage(c, n):
                if n == 3:
                    pe.wait_ge(s["hn_set"], c + 1)
                    for t in range(NT):
                        last = nc.tensor.transpose(pa[:, t * P:(t + 1) * P], hn[:, t, :], idf[:])
                    last.then_inc(s["hnT"], 1)
                elif n == 4:
                    pe.wait_ge(s["hnT_lo"], c + 1)
                    for k in range(ML):
                        w = slice(DI + k * P, DI + (k + 1) * P)
                        split((pb, pc)[k][:], (win_h[:, w], win_l[:, w]), hnT).then_inc(s["val_ps"], 1)
                    split(pa[:], (wz_h[:], wz_l[:]), hnT).then_inc(s["z_ps"], 1)
                elif n == 5:
                    for k in range(ML):
                        pe.wait_ge(s["v_sb"], c * ML + k + 1)
                        w = slice(k * P, (k + 1) * P)
                        split((pb, pc)[k][:], (win_h[:, w], win_l[:, w]), hnT).then_inc(s["gate_ps"], 1)
                elif n == 9:
                    pe.wait_ge(s["z_lo"], c * DC + DC)
                    pe.wait_ge(s["gate_sb"], c * ML + ML)
                    for k in range(ML):
                        w = slice(k * P, (k + 1) * P)
                        split((pb, pc)[k][:], (wa_h[:, w], wa_l[:, w]), (z_h[:], z_l[:]), stop=False)
                elif n == 11:
                    pe.wait_ge(s["s_lo"], c + 1)
                    for k in range(ML):
                        w = slice(k * P, (k + 1) * P)
                        for i in range(ML):
                            last = split((pb, pc)[k][:], (wb_h[:, i, w], wb_l[:, i, w]),
                                         (s_h[:, i, :], s_l[:, i, :]), start=False, stop=(i == ML - 1))
                        last.then_inc(s["y_ps"], 1)
                elif n == 13:
                    pe.wait_ge(s["g_lo"], c + 1)
                    for t in range(NT):
                        q = slice(t * P, (t + 1) * P)
                        for i in range(ML):
                            last = split(pa[:, t * D:(t + 1) * D], (g_h[:, i, q], g_l[:, i, q]),
                                         (wo_h[:, i, :], wo_l[:, i, :]), start=(i == 0), stop=(i == ML - 1))
                    last.then_inc(s["o_ps"], 1)
                elif n == 16:
                    pe.wait_ge(s["h2_set"], c * NT + NT)
                    for t in range(NT):
                        last = nc.tensor.transpose(pa[:, t * P:(t + 1) * P], h2[:, t, :], idf[:])
                    last.then_inc(s["h2T"], 1)
                    pe.wait_ge(s["h2T_lo"], c + 1)
                    for t in range(NT):
                        q = slice(t * P, (t + 1) * P)
                        last = split((pb, pc)[t // 2][:, t % 2 * E:(t % 2 + 1) * E], (nx_h[:, q], nx_l[:, q]),
                                     (wr_h[:], wr_l[:]))
                        if t % 2:
                            last.then_inc(s["lg_ps"], 1)
                    split(pa[0:INTER, :], (sg_h[:], sg_l[:]), nxT).then_inc(s["sh_up"], 1)
                elif n == 19:
                    pe.wait_ge(s["cn_set"], c + 1)
                    for t in range(NT):
                        nc.tensor.transpose(pb[:, t * P:(t + 1) * P], cw[:, t, 0:P], idf[:])
                        last = nc.tensor.transpose(pc[0:E - P, t * P:(t + 1) * P], cw[:, t, P:E], idf[:])
                    last.then_inc(s["cT"], 1)

            def down(c, i8, k, stop=False):
                lo_wait(pe, c, i8, k)
                w = bass.ds((i8 * BODY + k) * P, P)
                return split(acc_ps[:], (wd_h[:, w], wd_l[:, w]), (gw_h[:, k, :], gw_l[:, k, :]), start=False,
                             stop=stop)

            def products(c, i8, k, first):
                if first and k == 0:
                    pe.wait_ge(s["handed"], c * 2 + 2)
                if not first or k >= URING:
                    pe.wait_ge(s["silu_done"], count(c, i8, k - URING))
                w = bass.ds((i8 * BODY + k) * P, P)
                split(up_ps[k % URING][:], (wg_h[:, w], wg_l[:, w]), h2T).then_inc(s["up_ready"], 1)
                if first and k == LAG:
                    pe.wait_ge(s["sh_lo"], c + 1)
                    split(acc_ps[:], (sd_h[:], sd_l[:]), (ss_h[:], ss_l[:]), stop=False)
                if not first or k >= LAG:
                    down(c, *before(i8, k, LAG))

            def prologue():
                for n in range(GROUPS):
                    stage(0, n)
                pe.wait_ge(s["piece_lo"], 2 * NPIECE)

            def end(c):
                for k in range(BODY - LAG, BODY):
                    last = down(c, BLOCKS // BODY - 1, k, stop=(k == BODY - 1))
                last.then_inc(s["acc_ready"], 1)
                pe.wait_ge(s["acc_sb"], c + 1)
                for t in range(NT):
                    last = nc.tensor.transpose(pa[:, t * P:(t + 1) * P], accs[:, t * P:(t + 1) * P], idf[:])
                last.then_inc(s["accT"], 1)

            chunks(pe, prologue, products, stage, end)


_W = "L0_attn_"
_F = "L0_ffn_"


def kernel(**inputs):
    import numpy as np
    import concourse.bacc as bacc
    from concourse.bass_utils import run_bass_kernel_spmd

    a = {k: np.asarray(t) for k, t in inputs.items()}

    def blocks(t):
        return np.concatenate(np.split(t.reshape(t.shape[0], -1), t.shape[0] // P), 1)

    w = {k[len(_W):]: t for k, t in a.items() if k.startswith(_W)}
    f = {k[len(_F):]: t for k, t in a.items() if k.startswith(_F)}
    vecs = np.concatenate([blocks(t) for t in (
        w["norm_w"], w["in_b"], w["dwa_b"], w["sym_b"], w["pw_b"], w["fuse_b"], w["ha_b"], w["hb_b"],
        w["dwa_k"], w["sym_k"], w["A"], w["Bm"].T, a["L0_c"].T)], 1)
    mats = np.concatenate([blocks(t) for t in (
        a["L0_wmod"], w["in_w"].T, w["in_w"][DI:], w["ha_w"].T, w["hb_w"].T, w["pw_w"], w["fuse_w"].T, w["out_w"].T,
        f["router_w"].T, f["w_gate_shared"].T)], 1)
    rows = np.concatenate([f["expert_bias"], w["out_b"]])[None]
    wg = f["w_gate"].reshape(GROUPS, 2, 4, INTER, D).transpose(4, 0, 2, 3, 1).reshape(D, BLOCKS * P)
    wd = f["w_down"].reshape(GROUPS, 2, 4, D, INTER).transpose(4, 1, 0, 2, 3).reshape(P, BLOCKS * D)
    arrays = {"x": w["x"], "vecs": vecs, "mats": mats, "sdT": f["w_down_shared"].T, "rows": rows,
              "idf": np.eye(P, dtype=np.float32), "wg": wg, "wd": wd}
    arrays = {f"{k}_dram": np.ascontiguousarray(t) for k, t in arrays.items()}
    nc = bacc.Bacc("TRN2", target_bir_lowering=False, num_devices=1)
    args = [nc.dram_tensor(k, t.shape, mybir.dt.from_np(t.dtype), kind="ExternalInput").ap()
            for k, t in arrays.items()]
    out = nc.dram_tensor("out_dram", (B, L, D), F32, kind="ExternalOutput").ap()
    build(nc, *args, out)
    r = run_bass_kernel_spmd(nc, [arrays], core_ids=[0])
    return r.results[0]["out_dram"]
```

```python
from contextlib import ExitStack

import concourse.bass as bass
from concourse import mybir

F32 = mybir.dt.float32
F16 = mybir.dt.float16
BF16 = mybir.dt.bfloat16
ALU = mybir.AluOpType
ACT = mybir.ActivationFunctionType
AX = mybir.AxisListType

P = 128
B, L, D = 4, 512, 128
DI = 2 * D
ML = DI // P
DS, DC = 16, 4
KS = 2 * DC + 1
PADL = KS // 2
NT = L // P
E, TOPK, INTER = 160, 8, 64
ROUTED_SCALE = 2.5
BLOCKS = E // 2
BODY = 8
BODIES = BLOCKS // BODY
GROUPS = BLOCKS // 4
LAG = BODY - 1
URING = 4
SLOTS = (BLOCKS - BODY) // 2
SLOTB = 2
CSLOTS = 4
LOADS = BLOCKS // SLOTB
WS = 16.0
ES_SCALE = 64.0
PIECE = 8
NPIECE = BLOCKS // PIECE
STAGING = 4
HI_LAG = 2
PIECE_AT = (3, 3, 7, 8, 9, 17, 17, 17, 20, 20, 21, 24, 24, 28, 28, 30, 33, 33, 34, 34)
PIECE_DVE = {0: 5, 1: 5, 3: 15, 5: 18, 9: 21, 11: 26, 13: 28, 14: 29, 15: 33, 16: 33, 17: 33, 18: 34, 19: 34}

V = {}
_at = 0
for _n, _w in (("norm_w", 1), ("in_b", 4), ("dwa_b", ML), ("sym_b", ML), ("pw_b", ML), ("fuse_b", ML),
               ("ha_b", 1), ("hb_b", 1), ("dwa_k", ML * DC), ("sym_k", ML * KS), ("A", ML * DS), ("BmT", ML * DS),
               ("cT", B)):
    V[_n] = (_at, _w)
    _at += _w
NV = _at
M = {}
_at = 0
for _n, _w in (("wmod", 6 * D), ("in_wT", 2 * DI), ("inv", ML * D), ("haT", ML * P), ("hbT", ML * P),
               ("pw", ML * DI), ("fuseT", ML * DI), ("outT", ML * D), ("rT", E), ("sgT", INTER)):
    M[_n] = (_at, _w)
    _at += _w
NM = _at


def build(nc, x, vecs, mats, sdT, rows, idf_c, wg, wd, out):
    c_dram = nc.dram_tensor("combine", (B, E, L), F32, kind="Internal").ap()
    with ExitStack() as ctx:
        def sb(name, shape, dt=F32):
            return ctx.enter_context(nc.sbuf_tensor(name, shape, dt))

        def sem(name):
            return ctx.enter_context(nc.semaphore(name))

        bank = [ctx.enter_context(nc.psum_tensor(f"bank{i}", [P, 512], F32)) for i in range(8)]
        up_ps, acc_ps = bank[0:URING], bank[4]
        pa, pb, pc = bank[5], bank[6], bank[7]

        vec = sb("vec", [P, NV])
        mat = sb("mat", [P, NM])
        idf = sb("idf", [P, P])
        room = [0]

        def over_mat(shape, dt=F32):
            words = shape[0] * shape[1] * (2 if dt == F16 else 4) // 4
            ap = mat[:, room[0]:room[0] + words]
            room[0] += words
            assert room[0] <= NM
            ap = ap if dt == F32 else ap.bitcast(dt)
            return ap.rearrange("p (a b) -> p a b", a=shape[0])

        sdf = sb("sdf", [INTER, P])
        brow = sb("brow", [P, E + D])

        def v(name, i=0, n=1):
            at = V[name][0] + i
            return vec[:, at:at + n]

        def m(name, i=0, n=None):
            at, w = M[name]
            return mat[:, at + i:at + (w if n is None else i + n)]

        ebias, outb = brow[:, 0:E], brow[:, E:E + D]

        win_h, win_l = sb("win_h", [P, 2 * DI], F16), sb("win_l", [P, 2 * DI], F16)
        wz_h, wz_l = sb("wz_h", [P, P], F16), sb("wz_l", [P, P], F16)
        wa_h, wa_l = sb("wa_h", [P, DI], F16), sb("wa_l", [P, DI], F16)
        wb_h, wb_l = sb("wb_h", [P, ML, DI], F16), sb("wb_l", [P, ML, DI], F16)
        wo_h, wo_l = sb("wo_h", [P, ML, D], F16), sb("wo_l", [P, ML, D], F16)
        wr_h, wr_l = sb("wr_h", [P, E], F16), sb("wr_l", [P, E], F16)
        sg_h, sg_l = sb("sg_h", [P, INTER], F16), sb("sg_l", [P, INTER], F16)
        sd_h, sd_l = sb("sd_h", [INTER, P], F16), sb("sd_l", [INTER, P], F16)
        cbr = sb("cbr", [P, CSLOTS, SLOTB * L])
        jb, bz, by = sb("jb", [P, 1]), sb("bz", [P, 1]), sb("by", [P, ML])
        sct = sb("sct", [P, B])
        mod = sb("mod", [P, B, 6 * D])

        wg_h, wg_l = sb("wg_h", [P, BLOCKS * P], F16), sb("wg_l", [P, BLOCKS * P], F16)
        wd_h, wd_l = sb("wd_h", [P, BLOCKS * P], F16), sb("wd_l", [P, BLOCKS * P], F16)

        xt, h, x2, xf, ot, t1, hn = (sb(n, [P, NT, D]) for n in ("xt", "h", "x2", "xf", "ot", "t1", "hn"))
        base = xt
        hb, t2, h2 = (over_mat([NT, D]) for _ in range(3))
        xc2, t3 = t1, t2
        st, mv, st2, mv2 = sb("st", [P, NT, 6]), sb("mv", [P, NT, 2]), sb("st2", [P, NT, 6]), sb("mv2", [P, NT, 2])
        ve, rstd, ms, mse, rms = (sb(n, [P, NT]) for n in ("ve", "rstd", "ms", "mse", "rms"))
        ve2, rstd2 = sb("ve2", [P, NT]), sb("rstd2", [P, NT])
        mhalf, eps5, eps6 = (sb(n, [P, NT]) for n in ("mhalf", "eps5", "eps6"))
        hn_h, hn_l = sb("hn_h", [P, L], F16), sb("hn_l", [P, L], F16)
        vp = sb("vp", [P, ML, L + 2 * PADL])
        z_h, z_l = sb("z_h", [P, L], F16), sb("z_l", [P, L], F16)
        cv = sb("cv", [P, ML, L])
        sbv = cv
        s_h, s_l = over_mat([ML, L], F16), sb("s_l", [P, ML, L], F16)
        gate = sb("gate", [P, ML, L])
        gy = cv
        g_h, g_l = s_h, s_l
        h2_h, h2_l = sb("h2_h", [P, B, L], F16), sb("h2_l", [P, B, L], F16)

        def routes(t):
            return t[:].rearrange("p m l -> p (m l)")[:, 0:NT * E].rearrange("p (n e) -> p n e", n=NT)

        lg, pr, rp = routes(gate), over_mat([NT, E]), routes(cv)
        cw = lg
        mx = sb("mx", [P, NT, TOPK])
        sm, sme, rs = sb("sm", [P, NT]), sb("sme", [P, NT]), sb("rs", [P, NT])
        cT0, cT1 = (t.rearrange("p n d -> p (n d)") for t in (hb, h2))
        ss = h[0:INTER].rearrange("p n d -> p (n d)")
        ss_h, ss_l = sb("ss_h", [INTER, L], F16), sb("ss_l", [INTER, L], F16)
        gw = sb("gw", [P, BODY, L])
        gw_h, gw_l = sb("gw_h", [P, BODY, L], F16), sb("gw_l", [P, BODY, L], F16)
        accs = t1[:].rearrange("p n d -> p (n d)")
        sq = hn
        stage_sb = gw[:, 0:2 * STAGING].rearrange("p (a b) l -> p a (b l)", b=2)
        gmag, gsgn = (cbr[:, q].rearrange("p (b j d) -> p b j d", b=B, j=2) for q in (2, 3))
        gate_rows = mod[:].rearrange("p b (k j d) -> p b k j d", k=2, j=3)[:, :, :, 2, :]
        scb = cbr[:, 1, 384:384 + B * P].rearrange("p (b r) -> p b r", b=B)
        wf = cbr[:, 0, 0:640]
        gmat, qmat = cbr[:, 1, 0:P], cbr[:, 1, P:P + DI]
        ak, a1, bm4 = (cbr[:, 2, i * DI:(i + 1) * DI].rearrange("p (m k) -> p m k", m=ML) for i in range(3))

        s = {n: sem(n) for n in (
            "ld_idf ld_vec ld_wmod ld_mat ld_rows ld_sd x_loaded out_stored out_free ot_set cT_stored "
            "pads mhalf_set ak_set silu_c scb_set mod_ps mod_half mod_set gmag_set gsgn_set gates_set "
            "fold1 fold1_sb fold2 fold3 win_f win_hi win_lo wz_f wz_hi wz_lo wab_hi wab_lo wo_hi wo_lo "
            "jb_set bz_set by_set "
            "piece_scaled piece_hi piece_lo piece_lo_dve "
            "stats aggr ve_set rstd_set t1_set h_set sq_set mse_set rms_set hn_set hnT hnT_hi hnT_lo "
            "val_ps z_ps gate_ps v_sb z_hi z_lo conv0 conv1 gate_sb silu_b s_hi s_lo0 s_lo1 y_ps gy_set g_hi g_lo o_ps "
            "hb_set hg_set base_set t2_set x2_set stats2 aggr2 ve2_set rstd2_set xc2_set h2_set h2T h2T_hi h2T_lo "
            "lg_ps lg_set pr_set mx_set rp_set cw_set sm_set sme_set rs_set cn_set cT cT_sb xf_set "
            "sh_up sh_silu sh_hi sh_lo up_ready silu_done gw_done hi_done lo_done acc_ready acc_sb accT t3_set"
        ).split()}
        cb_landed = [sem(f"cb_landed{i}") for i in range(CSLOTS)]
        ld_piece = [sem(f"ld_piece{i}") for i in range(STAGING)]

        wpiece = [wg[:, i * PIECE * P:(i + 1) * PIECE * P] for i in range(NPIECE)] + \
                 [wd[:, i * PIECE * P:(i + 1) * PIECE * P] for i in range(NPIECE)]
        xv = x.rearrange("b (n p) d -> b p n d", p=P)
        ov = out.rearrange("b (n p) d -> b p n d", p=P)

        def bc(ap, n):
            return ap.rearrange("p (t o) -> p t o", o=1).broadcast_to([P, NT, n])

        def hid(t, c):
            return t[:, bass.ds(c, 1), :].rearrange("p a l -> p (a l)")

        def modr(c, j, k=NT):
            return mod[:, bass.ds(c, 1), j * D:(j + 1) * D].broadcast_to([P, k, D])

        def cached_wait(eng, sem_, c):
            eng.wait_ge(s["ld_vec"], 16)
            eng.wait_ge(sem_, c + 1)

        def count(c, i8, k):
            return c * BLOCKS + i8 * BODY + (k + 1)

        def before(i8, k, n):
            return (i8, k - n) if k >= n else (i8 - 1, k - n + BODY)

        def is_first(c, i8, k, n):
            return isinstance(c, int) and c == 0 and isinstance(i8, int) and i8 * BODY + k < n

        def pieces_after(n):
            return [i for i, at in enumerate(PIECE_AT) if at == n]

        def piece_wait(eng, i):
            on_dve = sum(j <= i for j in PIECE_DVE)
            if i in PIECE_DVE:
                eng.wait_ge(s["piece_lo_dve"], on_dve)
            else:
                eng.wait_ge(s["piece_lo"], i + 1 - on_dve)

        def chunks(eng, prologue, block, stage, end, finish):
            prologue()
            for k in range(BODY):
                block(0, 0, k)
            with eng.Fori(0, B - 1) as c:
                for n in range(SLOTS):
                    block(c, 1 + n // 4, n % 4 * 2)
                    block(c, 1 + n // 4, n % 4 * 2 + 1)
                    stage(c + 1, n)
                for k in range(BODY):
                    block(c, BODIES, k)
                end(c)
            with eng.Fori(1, BODIES) as i8:
                for k in range(BODY):
                    block(B - 1, i8, k)
            finish(B - 1)

        block = ctx.enter_context(nc.Block())

        @block.sync
        def _(sp):
            sp.dma_start(vec[:], vecs).then_inc(s["ld_vec"], 16)
            sp.dma_start(xt[:], xv[0]).then_inc(s["x_loaded"], 16)
            sp.dma_start(mat[:, 0:6 * D], mats[:, 0:6 * D]).then_inc(s["ld_wmod"], 16)
            sp.dma_start(mat[:, 6 * D:], mats[:, 6 * D:]).then_inc(s["ld_mat"], 16)
            sp.dma_start(sdf[:], sdT).then_inc(s["ld_sd"], 16)
            sp.dma_start(brow[:], rows.broadcast_to([P, E + D])).then_inc(s["ld_rows"], 16)
            sp.dma_start(idf[:], idf_c).then_inc(s["ld_idf"], 16)
            for i in range(2 * NPIECE):
                if i >= STAGING:
                    piece_wait(sp, i - STAGING)
                sp.dma_start(stage_sb[:, i % STAGING, :], wpiece[i]).then_inc(ld_piece[i % STAGING], 16)
            sp.sem_inc(s["out_free"], 1)

            def load_cb(c, j4, q):
                row = c_dram[bass.ds(c, 1)].rearrange("a (g h w) t -> a g h (w t)", h=2, w=4)
                g = j4 * 2 + q // 2
                src = row[:, bass.ds(g, 1), :, q % 2 * SLOTB * L:(q % 2 + 1) * SLOTB * L]\
                    .rearrange("a g h t -> (a g) h t").broadcast_to([INTER, 2, SLOTB * L])
                sp.dma_start(cbr[:, q, :], src).then_inc(cb_landed[q], 16)

            def body_cb(c, j4):
                for q in range(CSLOTS):
                    sp.wait_ge(s["gw_done"], count(c, j4 - 1, 2 * q + 1))
                    load_cb(c, j4, q)

            def store(c):
                sp.wait_ge(s["ot_set"], c + 1)
                sp.dma_start(ov[bass.ds(c, 1)].rearrange("a p n d -> (a p) n d"), ot[:]).then_inc(s["out_stored"], 16)

            sp.wait_ge(s["cT_stored"], 32)
            for q in range(CSLOTS):
                load_cb(0, 0, q)
            with sp.Fori(1, BODIES) as j4:
                body_cb(0, j4)
            with sp.Fori(1, B) as c:
                sp.wait_ge(s["cT_stored"], c * 32 + 32)
                for q in range(CSLOTS):
                    sp.wait_ge(s["gw_done"], count(c - 1, BODIES - 1, 2 * q + 1))
                    load_cb(c, 0, q)
                body_cb(c, 1)
                store(c - 1)
                with sp.Fori(2, BODIES) as j4:
                    body_cb(c, j4)
                sp.wait_ge(s["out_stored"], c * 16)
                sp.sem_inc(s["out_free"], 1)
            store(B - 1)
            sp.wait_ge(s["out_stored"], 16 * B)

        @block.gpsimd
        def _(pool):
            g = nc.gpsimd
            for t, value in ((mhalf, -0.5), (eps5, 1e-5), (eps6, 1e-6)):
                g.memset(t[:], value).then_inc(s["mhalf_set"], 1)
            pool.wait_ge(s["mhalf_set"], 3)
            for t in (ak, a1, bm4, vp[:], z_h[:], z_l[:]):
                g.memset(t, 0.0).then_inc(s["pads"], 1)

            def piece(i):
                at = slice(i % NPIECE * PIECE * P, (i % NPIECE + 1) * PIECE * P)
                hi, lo = ((wg_h, wg_l) if i < NPIECE else (wd_h, wd_l))
                pool.wait_ge(s["piece_hi"], i + 1)
                g.tensor_tensor(lo[:, at], stage_sb[:, i % STAGING, :], hi[:, at], ALU.subtract)\
                    .then_inc(s["piece_lo"], 1)

            def stage(c, n):
                if n == 0:
                    pool.wait_ge(s["aggr"], c + 1)
                    g.tensor_tensor(ve[:], mv[:, :, 1], eps5[:], ALU.add).then_inc(s["ve_set"], 1)
                    pool.wait_ge(s["ve_set"], c + 1)
                    g.tensor_tensor(rstd[:], ve[:], mhalf[:], ALU.pow).then_inc(s["rstd_set"], 1)
                elif n == 2:
                    pool.wait_ge(s["sq_set"], c + 1)
                    g.tensor_tensor(mse[:], ms[:], eps6[:], ALU.add).then_inc(s["mse_set"], 1)
                    pool.wait_ge(s["mse_set"], c + 1)
                    g.tensor_tensor(rms[:], mse[:], mhalf[:], ALU.pow).then_inc(s["rms_set"], 1)
                elif n == 13:
                    pool.wait_ge(s["s_hi"], c * ML + 1)
                    g.tensor_tensor(s_l[:, 0, :], sbv[:, 0, :], s_h[:, 0, :], ALU.subtract).then_inc(s["s_lo0"], 1)
                elif n == 17:
                    g.tensor_tensor(hb[:], h[:], outb.rearrange("p (o d) -> p o d", o=1).broadcast_to([P, NT, D]),
                                    ALU.add).then_inc(s["hb_set"], 1)
                elif n == 19:
                    pool.wait_ge(s["gates_set"], 1)
                    pool.wait_ge(s["hb_set"], c + 1)
                    g.tensor_tensor(hb[:], hb[:], modr(c, 2), ALU.mult).then_inc(s["hg_set"], 1)
                elif n == 20:
                    pool.wait_ge(s["hg_set"], c + 1)
                    g.tensor_tensor(base[:], hb[:], xt[:], ALU.add).then_inc(s["base_set"], 1)
                elif n == 23:
                    pool.wait_ge(s["aggr2"], c + 1)
                    g.tensor_tensor(ve2[:], mv2[:, :, 1], eps5[:], ALU.add).then_inc(s["ve2_set"], 1)
                    pool.wait_ge(s["ve2_set"], c + 1)
                    g.tensor_tensor(rstd2[:], ve2[:], mhalf[:], ALU.pow).then_inc(s["rstd2_set"], 1)

            def low(c, i8, k):
                pool.wait_ge(s["hi_done"], count(c, i8, k))
                g.tensor_tensor(gw_l[:, k, :], gw[:, k, :], gw_h[:, k, :], ALU.subtract).then_inc(s["lo_done"], 1)

            def prologue():
                for n in range(SLOTS):
                    if n == 17:
                        pool.wait_ge(s["mod_half"], 2 * B)
                        g.tensor_scalar(gsgn, gate_rows, 0.0, None, ALU.is_ge).then_inc(s["gsgn_set"], 1)
                        pool.wait_ge(s["gsgn_set"], 1)
                        g.tensor_scalar(gsgn, gsgn, 2.0, -1.0, ALU.mult, ALU.add).then_inc(s["gsgn_set"], 1)
                        pool.wait_ge(s["ld_rows"], 16)
                        pool.wait_ge(s["gmag_set"], 1)
                    stage(0, n)
                    for i in pieces_after(n):
                        if i not in PIECE_DVE:
                            piece(i)

            chunks(pool, prologue, low, stage, lambda c: None, lambda c: None)

        @block.scalar
        def _(act):
            a = nc.scalar.activation

            def rows_of(b):
                act.wait_ge(s["mod_ps"], 2 * b + 1)
                a(mod[:, b, 0:512], up_ps[0][:], ACT.Copy).then_inc(s["mod_half"], 1)
                act.wait_ge(s["mod_ps"], 2 * b + 2)
                a(mod[:, b, 512:768], up_ps[1][:, 0:256], ACT.Copy).then_inc(s["mod_half"], 1)

            def piece(i):
                dst = (wg_h if i < NPIECE else wd_h)[:, i % NPIECE * PIECE * P:(i % NPIECE + 1) * PIECE * P]
                src = stage_sb[:, i % STAGING]
                act.wait_ge(ld_piece[i % STAGING], 16 * (i // STAGING + 1))
                if i in PIECE_DVE:
                    a(dst, src, ACT.Copy, scale=ES_SCALE).then_inc(s["piece_hi"], 1)
                else:
                    a(src, src, ACT.Copy, scale=ES_SCALE).then_inc(s["piece_scaled"], 1)
                    act.wait_ge(s["piece_scaled"], i + 1 - sum(j <= i for j in PIECE_DVE))
                    a(dst, src, ACT.Copy).then_inc(s["piece_hi"], 1)

            def setup(n):
                if n == 0:
                    act.wait_ge(s["ld_vec"], 16)
                    a(sct[:], v("cT", 0, B), ACT.Silu).then_inc(s["silu_c"], 1)
                    rows_of(0)
                elif n == 3:
                    act.wait_ge(s["win_f"], 1)
                    a(win_h[:], wf[:, 0:2 * DI], ACT.Copy).then_inc(s["win_hi"], 1)
                elif n == 7:
                    act.wait_ge(s["ld_mat"], 16)
                    a(wo_h[:].rearrange("p m d -> p (m d)"), m("outT"), ACT.Copy, scale=WS).then_inc(s["wo_hi"], 1)
                    a(wr_h[:], m("rT"), ACT.Copy, scale=ES_SCALE).then_inc(s["wo_hi"], 1)
                    a(sg_h[:], m("sgT"), ACT.Copy, scale=ES_SCALE).then_inc(s["wo_hi"], 1)
                    act.wait_ge(s["ld_sd"], 16)
                    a(sd_h[:], sdf[:], ACT.Copy, scale=ES_SCALE).then_inc(s["wo_hi"], 1)
                elif n == 8:
                    act.wait_ge(s["wz_f"], 1)
                    a(wz_h[:], wf[:, 512:640], ACT.Copy).then_inc(s["wz_hi"], 1)
                elif n == 11:
                    rows_of(1)
                elif n == 13:
                    rows_of(2)
                    act.wait_ge(s["fold3"], 1)
                    a(wa_h[:], up_ps[2][:, 0:DI], ACT.Copy).then_inc(s["wab_hi"], 1)
                    act.wait_ge(s["fold3"], 2)
                    a(wb_h[:].rearrange("p m o -> p (m o)"), up_ps[3][:], ACT.Copy, scale=WS).then_inc(s["wab_hi"], 1)
                elif n == 17:
                    rows_of(3)
                    act.wait_ge(s["mod_half"], 2 * B)
                    a(gmag, gate_rows, ACT.Abs).then_inc(s["gmag_set"], 1)

            def stage(c, n):
                if n == 2:
                    for t in range(NT):
                        act.wait_ge(s["h_set"], c * NT + t + 1)
                        last = a(sq[:, t, :], h[:, t, :], ACT.Square, scale=D ** -0.5, accum_out=ms[:, t:t + 1])
                    last.then_inc(s["sq_set"], 1)
                elif n == 5:
                    act.wait_ge(s["hnT"], c + 1)
                    a(hn_h[:], pa[:], ACT.Copy).then_inc(s["hnT_hi"], 1)
                elif n == 7:
                    for k in range(ML):
                        act.wait_ge(s["val_ps"], c * ML + k + 1)
                        a(vp[:, k, PADL:PADL + L], (pb, pc)[k][:], ACT.Identity, bias=v("in_b", ML + k),
                          scale=1.0 / WS).then_inc(s["v_sb"], 1)
                elif n in (8, 9):
                    act.wait_ge(s["z_ps"], c + 1)
                    for k in (2 * n - 16, 2 * n - 15):
                        lo, hi = max(0, 1 - k), min(L, L + 1 - k)
                        q = slice(32 * k, 32 * k + 32)
                        a(z_h[q, lo:hi], pa[q, lo + k - 1:hi + k - 1], ACT.Identity, bias=bz[q, 0:1])\
                            .then_inc(s["z_hi"], 1)
                elif n == 10:
                    for k in range(ML):
                        act.wait_ge(s["gate_ps"], c * ML + k + 1)
                        a(gate[:, k, :], (pb, pc)[k][:], ACT.Sigmoid, bias=v("in_b", k), scale=1.0 / WS)\
                            .then_inc(s["gate_sb"], 1)
                elif n in (12, 16):
                    k = (n - 12) // 4
                    act.wait_ge(s[f"conv{k}"], c * KS + KS)
                    a(sbv[:, k, :], cv[:, k, :], ACT.Silu).then_inc(s["silu_b"], 1)
                    act.wait_ge(s["silu_b"], c * ML + k + 1)
                    a(s_h[:, k, :], sbv[:, k, :], ACT.Copy).then_inc(s["s_hi"], 1)
                elif n == 27:
                    act.wait_ge(s["h2T"], c + 1)
                    a(hid(h2_h, c), pa[:], ACT.Copy).then_inc(s["h2T_hi"], 1)
                elif n == 30:
                    act.wait_ge(s["lg_set"], c * 2 + 2)
                    a(pr, lg, ACT.Sigmoid).then_inc(s["pr_set"], 1)
                elif n == 31:
                    act.wait_ge(s["sh_up"], c + 1)
                    a(ss, pa[0:INTER, :], ACT.Silu, scale=1.0 / ES_SCALE).then_inc(s["sh_silu"], 1)
                    act.wait_ge(s["sh_silu"], c + 1)
                    a(ss_h[:], ss, ACT.Copy).then_inc(s["sh_hi"], 1)
                elif n == 34:
                    act.wait_ge(s["cT"], c + 1)
                    a(cT0, pb[:], ACT.Copy).then_inc(s["cT_sb"], 1)
                    a(cT1[0:E - P, :], pc[0:E - P, :], ACT.Copy).then_inc(s["cT_sb"], 1)
                    act.wait_ge(s["cT_sb"], c * 2 + 2)
                    dst = c_dram[bass.ds(c, 1)].rearrange("a e t -> (a e) t")
                    act.dma_start(dst[0:P, :], cT0).then_inc(s["cT_stored"], 16)
                    act.dma_start(dst[P:E, :], cT1[0:E - P, :]).then_inc(s["cT_stored"], 16)

            def high(c, i8, k):
                act.wait_ge(s["gw_done"], count(c, i8, k))
                a(gw_h[:, k, :], gw[:, k, :], ACT.Copy).then_inc(s["hi_done"], 1)

            def sums(c):
                act.wait_ge(s["acc_ready"], c + 1)
                a(accs, acc_ps[:], ACT.Copy, scale=1.0 / ES_SCALE).then_inc(s["acc_sb"], 1)

            def hidden(c, i8, k):
                if isinstance(i8, int) and i8 == BODIES and k == LAG - 2:
                    sums(c)
                if is_first(c, i8, k, BODY) and k % 2 == 0:
                    piece_wait(act, 2 * NPIECE - STAGING + k // 2)
                act.wait_ge(s["up_ready"], count(c, i8, k))
                a(gw[:, k, :], up_ps[k % URING][:], ACT.Silu, scale=1.0 / ES_SCALE).then_inc(s["silu_done"], 1)
                if not is_first(c, i8, k, HI_LAG):
                    high(c, *before(i8, k, HI_LAG))
                if isinstance(i8, int) and i8 == 1 and k == 0:
                    act.wait_ge(s["x2_set"], c + 1)
                    act.dma_start(xt[:], xv[bass.ds(c + 1, 1)].rearrange("a p n d -> (a p) n d"))\
                        .then_inc(s["x_loaded"], 16)

            def prologue():
                for n in range(SLOTS):
                    setup(n)
                    stage(0, n)
                    for i in pieces_after(n):
                        piece(i)

            def finish(c):
                for k in range(BODY - HI_LAG, BODY):
                    high(c, BODIES - 1, k)
                sums(c)

            chunks(act, prologue, hidden, stage, lambda c: None, finish)

        @block.vector
        def _(dve):
            e = nc.vector

            def add_one(b):
                for j in (1, 4):
                    dve.wait_ge(s["mod_half"], 2 * b + (2 if j == 4 else 1))
                    r = mod[:, b, j * D:(j + 1) * D]
                    e.tensor_scalar(r, r, 1.0, None, ALU.add).then_inc(s["mod_set"], 1)

            def gates():
                dve.wait_ge(s["gmag_set"], 1)
                e.tensor_scalar(gmag, gmag, 0.25, None, ALU.max).then_inc(s["gmag_set"], 1)
                dve.wait_ge(s["gsgn_set"], 2)
                dve.wait_ge(s["gmag_set"], 2)
                e.tensor_tensor(gate_rows, gsgn, gmag, ALU.mult).then_inc(s["gates_set"], 1)

            def setup(n):
                if n == 0:
                    dve.wait_ge(s["silu_c"], 1)
                    e.tensor_copy(scb[:], sct[:].rearrange("p (b o) -> p b o", o=1).broadcast_to([P, B, P]))\
                        .then_inc(s["scb_set"], 1)
                    dve.wait_ge(s["ld_vec"], 16)
                    dve.wait_ge(s["pads"], 6)
                    for mm in range(ML):
                        for k in range(DC):
                            e.tensor_scalar(ak[:, mm, 32 * k:32 * k + DS], v("A", mm * DS, DS),
                                            v("dwa_k", mm * DC + k), None, ALU.mult).then_inc(s["ak_set"], 1)
                            e.tensor_copy(bm4[:, mm, 32 * k:32 * k + DS], v("BmT", mm * DS, DS))\
                                .then_inc(s["ak_set"], 1)
                        e.tensor_copy(a1[:, mm, 32:32 + DS], v("A", mm * DS, DS)).then_inc(s["ak_set"], 1)
                elif n == 1:
                    add_one(0)
                    dve.wait_ge(s["mod_set"], 2)
                elif n == 2:
                    dve.wait_ge(s["ld_mat"], 16)
                    e.tensor_scalar(wf[:, 0:2 * DI], m("in_wT"), v("norm_w"), WS, ALU.mult, ALU.mult)\
                        .then_inc(s["win_f"], 1)
                elif n == 4:
                    dve.wait_ge(s["win_hi"], 1)
                    e.tensor_tensor(win_l[:], wf[:, 0:2 * DI], win_h[:], ALU.subtract).then_inc(s["win_lo"], 1)
                    dve.wait_ge(s["fold1"], 1)
                    e.tensor_copy(gmat[:], pc[:, 0:P]).then_inc(s["fold1_sb"], 1)
                    e.tensor_copy(qmat[:], pc[:, P:P + DI]).then_inc(s["fold1_sb"], 1)
                    e.tensor_tensor(jb[:], pc[:, 384:385], v("hb_b"), ALU.add).then_inc(s["jb_set"], 1)
                elif n == 8:
                    dve.wait_ge(s["fold2"], 1)
                    e.tensor_scalar(wf[:, 512:640], acc_ps[:, 0:P], v("norm_w"), WS, ALU.mult, ALU.mult)\
                        .then_inc(s["wz_f"], 1)
                    e.tensor_scalar(bz[:], acc_ps[:, 128:129], WS, None, ALU.mult).then_inc(s["bz_set"], 1)
                elif n == 9:
                    dve.wait_ge(s["wz_hi"], 1)
                    e.tensor_tensor(wz_l[:], wf[:, 512:640], wz_h[:], ALU.subtract).then_inc(s["wz_lo"], 1)
                elif n == 16:
                    for i, (hi, src, lo) in enumerate(((wo_h[:].rearrange("p m d -> p (m d)"), m("outT"),
                                                        wo_l[:].rearrange("p m d -> p (m d)")),
                                                       (wr_h[:], m("rT"), wr_l[:]), (sg_h[:], m("sgT"), sg_l[:]),
                                                       (sd_h[:], sdf[:], sd_l[:]))):
                        dve.wait_ge(s["wo_hi"], i + 1)
                        e.scalar_tensor_tensor(out=lo, in0=src, scalar=WS if i == 0 else ES_SCALE, in1=hi,
                                               op0=ALU.mult, op1=ALU.subtract).then_inc(s["wo_lo"], 1)
                    dve.wait_ge(s["wab_hi"], 1)
                    e.tensor_tensor(wa_l[:], up_ps[2][:, 0:DI], wa_h[:], ALU.subtract).then_inc(s["wab_lo"], 1)
                    dve.wait_ge(s["wab_hi"], 2)
                    e.scalar_tensor_tensor(out=wb_l[:].rearrange("p m o -> p (m o)"), in0=up_ps[3][:], scalar=WS,
                                           in1=wb_h[:].rearrange("p m o -> p (m o)"), op0=ALU.mult,
                                           op1=ALU.subtract).then_inc(s["wab_lo"], 1)
                    e.tensor_tensor(by[:], up_ps[2][:, 256:256 + ML], v("fuse_b", 0, ML), ALU.add)\
                        .then_inc(s["by_set"], 1)
                    dve.wait_ge(s["by_set"], 1)
                    e.tensor_scalar(by[:], by[:], WS, None, ALU.mult).then_inc(s["by_set"], 1)
                elif n == 19:
                    gates()
                    dve.wait_ge(s["by_set"], 2)
                elif n == 22:
                    for b in range(1, B):
                        add_one(b)
                    dve.wait_ge(s["gates_set"], 1)
                    dve.wait_ge(s["ld_rows"], 16)

            def piece(i):
                at = slice(i % NPIECE * PIECE * P, (i % NPIECE + 1) * PIECE * P)
                hi, lo = ((wg_h, wg_l) if i < NPIECE else (wd_h, wd_l))
                dve.wait_ge(s["piece_hi"], i + 1)
                e.scalar_tensor_tensor(out=lo[:, at], in0=stage_sb[:, i % STAGING, :], scalar=ES_SCALE, in1=hi[:, at],
                                       op0=ALU.mult, op1=ALU.subtract).then_inc(s["piece_lo_dve"], 1)

            def row(c, j):
                return mod[:, bass.ds(c, 1), j * D:(j + 1) * D].rearrange("p a d -> p (a d)")

            def conv(c, mm, k):
                src = vp[:, mm, k:k + L]
                if k == 0:
                    dve.wait_ge(s["v_sb"], c * ML + mm + 1)
                    e.tensor_scalar(cv[:, mm, :], src, v("sym_k", mm * KS), v("sym_b", mm), ALU.mult, ALU.add)\
                        .then_inc(s[f"conv{mm}"], 1)
                else:
                    dve.wait_ge(s[f"conv{mm}"], c * KS + k)
                    e.scalar_tensor_tensor(out=cv[:, mm, :], in0=src, scalar=v("sym_k", mm * KS + k),
                                           in1=cv[:, mm, :], op0=ALU.mult, op1=ALU.add).then_inc(s[f"conv{mm}"], 1)

            def rests(c, *taps):
                for k in taps:
                    lo, hi = max(0, 1 - k), min(L, L + 1 - k)
                    q = slice(32 * k, 32 * k + 32)
                    dve.wait_ge(s["z_hi"], c * DC + k + 1)
                    e.scalar_tensor_tensor(out=z_l[q, lo:hi], in0=pa[q, lo + k - 1:hi + k - 1], scalar=bz[q, 0:1],
                                           in1=z_h[q, lo:hi], op0=ALU.add, op1=ALU.subtract).then_inc(s["z_lo"], 1)

            def stage(c, n):
                if n == 0:
                    dve.wait_ge(s["x_loaded"], c * 16 + 16)
                    dve.wait_ge(s["pads"], c + 1)
                    for t in range(NT):
                        last = e.bn_stats(st[:, t, :], xt[:, t, :])
                    last.then_inc(s["stats"], 1)
                    cached_wait(dve, s["stats"], c)
                    for t in range(NT):
                        last = e.bn_aggr(mv[:, t, :], st[:, t, :])
                    last.then_inc(s["aggr"], 1)
                elif n == 1:
                    dve.wait_ge(s["aggr"], c + 1)
                    for t in range(NT):
                        e.scalar_tensor_tensor(out=t1[:, t, :], in0=xt[:, t, :], scalar=mv[:, t, 0:1], in1=row(c, 1),
                                               op0=ALU.subtract, op1=ALU.mult).then_inc(s["t1_set"], 1)
                    dve.wait_ge(s["rstd_set"], c + 1)
                    for t in range(NT):
                        dve.wait_ge(s["t1_set"], c * NT + t + 1)
                        e.scalar_tensor_tensor(out=h[:, t, :], in0=t1[:, t, :], scalar=rstd[:, t:t + 1],
                                               in1=row(c, 0), op0=ALU.mult, op1=ALU.add).then_inc(s["h_set"], 1)
                elif n == 3:
                    dve.wait_ge(s["rms_set"], c + 1)
                    e.tensor_tensor(hn[:], h[:], bc(rms[:], D), ALU.mult).then_inc(s["hn_set"], 1)
                elif n == 5:
                    dve.wait_ge(s["hnT_hi"], c + 1)
                    e.tensor_tensor(hn_l[:], pa[:], hn_h[:], ALU.subtract).then_inc(s["hnT_lo"], 1)
                elif 7 <= n < 7 + KS:
                    for i in (2 * n - 14, 2 * n - 13):
                        conv(c, i // KS, i % KS)
                elif n == 16:
                    rests(c, 0)
                    dve.wait_ge(s["s_hi"], c * ML + ML)
                    e.tensor_tensor(s_l[:, 1, :], sbv[:, 1, :], s_h[:, 1, :], ALU.subtract).then_inc(s["s_lo1"], 1)
                elif n == 17:
                    rests(c, 1, 2)
                elif n == 18:
                    rests(c, 3)
                elif n in (19, 20):
                    k = n - 19
                    dve.wait_ge(s["gate_sb"], c * ML + ML)
                    dve.wait_ge(s["y_ps"], c * ML + k + 1)
                    e.scalar_tensor_tensor(out=gy[:, k, :], in0=(pb, pc)[k][:], scalar=by[:, k:k + 1],
                                           in1=gate[:, k, :], op0=ALU.add, op1=ALU.mult).then_inc(s["gy_set"], 1)
                elif n == 21:
                    dve.wait_ge(s["gy_set"], c * ML + ML)
                    e.tensor_copy(g_h, gy[:]).then_inc(s["g_hi"], 1)
                    dve.wait_ge(s["g_hi"], c + 1)
                    e.tensor_tensor(g_l[:], gy[:], g_h, ALU.subtract).then_inc(s["g_lo"], 1)
                elif n == 23:
                    dve.wait_ge(s["o_ps"], c + 1)
                    e.scalar_tensor_tensor(out=t2[:], in0=pa[:].rearrange("p (n d) -> p n d", d=D),
                                           scalar=1.0 / (WS * WS), in1=modr(c, 2), op0=ALU.mult, op1=ALU.mult)\
                        .then_inc(s["t2_set"], 1)
                    if not isinstance(c, int):
                        dve.wait_ge(s["xf_set"], c)
                    dve.wait_ge(s["base_set"], c + 1)
                    dve.wait_ge(s["t2_set"], c + 1)
                    e.tensor_tensor(x2[:], t2[:], base[:], ALU.add).then_inc(s["x2_set"], 1)
                    dve.wait_ge(s["x2_set"], c + 1)
                    for t in range(NT):
                        last = e.bn_stats(st2[:, t, :], x2[:, t, :])
                    last.then_inc(s["stats2"], 1)
                    cached_wait(dve, s["stats2"], c)
                    for t in range(NT):
                        last = e.bn_aggr(mv2[:, t, :], st2[:, t, :])
                    last.then_inc(s["aggr2"], 1)
                elif n == 24:
                    dve.wait_ge(s["aggr2"], c + 1)
                    for t in range(NT):
                        e.scalar_tensor_tensor(out=xc2[:, t, :], in0=x2[:, t, :], scalar=mv2[:, t, 0:1],
                                               in1=row(c, 4), op0=ALU.subtract, op1=ALU.mult)\
                            .then_inc(s["xc2_set"], 1)
                elif n == 25:
                    dve.wait_ge(s["rstd2_set"], c + 1)
                    for t in range(NT):
                        dve.wait_ge(s["xc2_set"], c * NT + t + 1)
                        e.scalar_tensor_tensor(out=h2[:, t, :], in0=xc2[:, t, :], scalar=rstd2[:, t:t + 1],
                                               in1=row(c, 3), op0=ALU.mult, op1=ALU.add).then_inc(s["h2_set"], 1)
                elif n == 27:
                    dve.wait_ge(s["h2T_hi"], c + 1)
                    e.tensor_tensor(hid(h2_l, c), pa[:], hid(h2_h, c), ALU.subtract).then_inc(s["h2T_lo"], 1)
                elif n == 29:
                    for k in range(2):
                        dve.wait_ge(s["lg_ps"], c * 2 + k + 1)
                        e.scalar_tensor_tensor(
                            out=lg[:, 2 * k:2 * k + 2, :],
                            in0=(pb, pc)[k][:, 0:2 * E].rearrange("p (n e) -> p n e", n=2), scalar=1.0 / ES_SCALE,
                            in1=ebias.rearrange("p (o e) -> p o e", o=1).broadcast_to([P, 2, E]), op0=ALU.mult,
                            op1=ALU.add).then_inc(s["lg_set"], 1)
                elif n == 31:
                    cached_wait(dve, s["pr_set"], c)
                    for t in range(NT):
                        last = e.max(mx[:, t, :], pr[:, t, :])
                    last.then_inc(s["mx_set"], 1)
                    cached_wait(dve, s["mx_set"], c)
                    for t in range(NT):
                        last = e.match_replace(rp[:, t, :], mx[:, t, :], pr[:, t, :], 0.0)
                    last.then_inc(s["rp_set"], 1)
                elif n == 32:
                    e.tensor_reduce(sm[:], mx[:], AX.X, ALU.add).then_inc(s["sm_set"], 1)
                    dve.wait_ge(s["rp_set"], c + 1)
                    e.tensor_tensor(cw, pr, rp, ALU.subtract).then_inc(s["cw_set"], 1)
                    dve.wait_ge(s["sm_set"], c + 1)
                    e.tensor_scalar(sme[:], sm[:], 1e-9, 1.0 / ROUTED_SCALE, ALU.add, ALU.mult)\
                        .then_inc(s["sme_set"], 1)
                    dve.wait_ge(s["sme_set"], c + 1)
                    e.reciprocal(rs[:], sme[:]).then_inc(s["rs_set"], 1)
                    dve.wait_ge(s["rs_set"], c + 1)
                    dve.wait_ge(s["cw_set"], c + 1)
                    e.tensor_tensor(cw, cw, bc(rs[:], E), ALU.mult).then_inc(s["cn_set"], 1)
                elif n == 33:
                    dve.wait_ge(s["sh_hi"], c + 1)
                    e.tensor_tensor(ss_l[:], ss, ss_h[:], ALU.subtract).then_inc(s["sh_lo"], 1)

            def weigh(c, i8, k):
                dve.wait_ge(s["silu_done"], count(c, i8, k))
                dve.wait_ge(cb_landed[k // 2], c * (16 * LOADS // CSLOTS) + i8 * 16 + 16)
                e.tensor_tensor(gw[:, k, :], gw[:, k, :], cbr[:, k // 2, k % 2 * L:(k % 2 + 1) * L], ALU.mult)\
                    .then_inc(s["gw_done"], 1)

            def prologue():
                for n in range(SLOTS):
                    setup(n)
                    stage(0, n)
                    for i, at in PIECE_DVE.items():
                        if at == n:
                            piece(i)
                e.tensor_copy(xf[:], x2[:]).then_inc(s["xf_set"], 1)

            def result(c):
                dve.wait_ge(s["accT"], c + 1)
                e.tensor_tensor(t3[:], pa[:].rearrange("p (n d) -> p n d", d=D), modr(c, 5), ALU.mult)\
                    .then_inc(s["t3_set"], 1)
                dve.wait_ge(s["out_free"], c + 1)
                dve.wait_ge(s["t3_set"], c + 1)
                e.tensor_tensor(ot[:], t3[:], xf[:], ALU.add).then_inc(s["ot_set"], 1)

            def end(c):
                result(c)
                dve.wait_ge(s["ot_set"], c + 1)
                e.tensor_copy(xf[:], x2[:]).then_inc(s["xf_set"], 1)

            chunks(dve, prologue, weigh, stage, end, result)

        @block.tensor
        def _(pe):
            mm = nc.tensor.matmul

            def split(dst, lhs, rhs, start=True, stop=True):
                (lh, ll), (rh, rl) = lhs, rhs
                mm(dst, lh, rh, start=start, stop=False)
                mm(dst, ll, rh, start=False, stop=False)
                return mm(dst, lh, rl, start=False, stop=stop)

            def rows_of(b):
                if b:
                    pe.wait_ge(s["mod_half"], 2 * b)
                mm(up_ps[0][:], scb[:, b, :], m("wmod", 0, 512)).then_inc(s["mod_ps"], 1)
                mm(up_ps[1][:, 0:256], scb[:, b, :], m("wmod", 512, 256)).then_inc(s["mod_ps"], 1)

            def setup(n):
                if n == 0:
                    pe.wait_ge(s["ld_wmod"], 16)
                    pe.wait_ge(s["scb_set"], 1)
                    rows_of(0)
                    pe.wait_ge(s["ld_mat"], 16)
                    pe.wait_ge(s["ak_set"], ML * (2 * DC + 1))
                    for k in range(ML):
                        mm(pc[:, 0:P], m("haT", k * P, P), bm4[:, k, :], start=(k == 0), stop=(k == ML - 1))
                    for k in range(ML):
                        mm(pc[:, P:P + DI], m("hbT", k * P, P), m("pw", k * DI, DI), start=(k == 0),
                           stop=(k == ML - 1))
                    for k in range(ML):
                        last = mm(pc[:, 384:385], m("hbT", k * P, P), v("pw_b", k), start=(k == 0),
                                  stop=(k == ML - 1))
                    last.then_inc(s["fold1"], 1)
                    pe.wait_ge(s["ld_idf"], 16)
                elif n == 7:
                    pe.wait_ge(s["win_lo"], 1)
                elif n == 8:
                    for k in range(ML):
                        mm(acc_ps[:, 0:P], m("inv", k * D, D), ak[:, k, :], start=(k == 0), stop=(k == ML - 1))
                    for k in range(ML):
                        mm(acc_ps[:, 128:129], ak[:, k, :], v("in_b", ML + k), start=(k == 0), stop=False)
                    for k in range(ML):
                        last = mm(acc_ps[:, 128:129], a1[:, k, :], v("dwa_b", k), start=False, stop=(k == ML - 1))
                    last.then_inc(s["fold2"], 1)
                elif n == 9:
                    pe.wait_ge(s["fold1_sb"], 2)
                    pe.wait_ge(s["jb_set"], 1)
                    mm(up_ps[2][:, 0:DI], gmat[:], m("fuseT", 0, DI))
                    for k in range(ML):
                        mm(up_ps[2][:, 256 + k:257 + k], m("fuseT", k * P, P), v("ha_b"), start=True, stop=False)
                        last = mm(up_ps[2][:, 256 + k:257 + k], m("fuseT", DI + k * P, P), jb[:], start=False,
                                  stop=True)
                    last.then_inc(s["fold3"], 1)
                    for k in range(ML):
                        last = mm(up_ps[3][:, k * DI:(k + 1) * DI], qmat[:, k * P:(k + 1) * P], m("fuseT", DI, DI))
                    last.then_inc(s["fold3"], 1)
                    for b in range(1, B):
                        rows_of(b)
                elif n == 17:
                    pe.wait_ge(s["wab_lo"], 2)
                    pe.wait_ge(s["by_set"], 1)
                elif n == 22:
                    pe.wait_ge(s["wo_lo"], 4)

            hnT = (hn_h[:], hn_l[:])

            def stage(c, n):
                if n == 5:
                    pe.wait_ge(s["hn_set"], c + 1)
                    for t in range(NT):
                        last = nc.tensor.transpose(pa[:, t * P:(t + 1) * P], hn[:, t, :], idf[:])
                    last.then_inc(s["hnT"], 1)
                elif n == 7:
                    pe.wait_ge(s["hnT_lo"], c + 1)
                    for k in range(ML):
                        w = slice(DI + k * P, DI + (k + 1) * P)
                        split((pb, pc)[k][:], (win_h[:, w], win_l[:, w]), hnT).then_inc(s["val_ps"], 1)
                elif n == 8:
                    for k in range(ML):
                        pe.wait_ge(s["v_sb"], c * ML + k + 1)
                        w = slice(k * P, (k + 1) * P)
                        split((pb, pc)[k][:], (win_h[:, w], win_l[:, w]), hnT).then_inc(s["gate_ps"], 1)
                    pe.wait_ge(s["wz_lo"], 1)
                    split(pa[:], (wz_h[:], wz_l[:]), hnT).then_inc(s["z_ps"], 1)
                elif n == 17:
                    pe.wait_ge(s["gate_sb"], c * ML + ML)
                    pe.wait_ge(s["s_lo0"], c + 1)
                    for k in range(ML):
                        w = slice(k * P, (k + 1) * P)
                        split((pb, pc)[k][:], (wb_h[:, 0, w], wb_l[:, 0, w]), (s_h[:, 0, :], s_l[:, 0, :]), stop=False)
                elif n == 19:
                    pe.wait_ge(s["s_lo1"], c + 1)
                    for k in range(ML):
                        w = slice(k * P, (k + 1) * P)
                        split((pb, pc)[k][:], (wb_h[:, 1, w], wb_l[:, 1, w]), (s_h[:, 1, :], s_l[:, 1, :]),
                              start=False, stop=False)
                    pe.wait_ge(s["z_lo"], c * DC + DC)
                    for k in range(ML):
                        w = slice(k * P, (k + 1) * P)
                        split((pb, pc)[k][:], (wa_h[:, w], wa_l[:, w]), (z_h[:], z_l[:]), start=False)\
                            .then_inc(s["y_ps"], 1)
                elif n == 23:
                    pe.wait_ge(s["g_lo"], c + 1)
                    for t in range(NT):
                        q = slice(t * P, (t + 1) * P)
                        for i in range(ML):
                            last = split(pa[:, t * D:(t + 1) * D], (g_h[:, i, q], g_l[:, i, q]),
                                         (wo_h[:, i, :], wo_l[:, i, :]), start=(i == 0), stop=(i == ML - 1))
                    last.then_inc(s["o_ps"], 1)
                elif n == 27:
                    pe.wait_ge(s["h2_set"], c * NT + NT)
                    for t in range(NT):
                        last = nc.tensor.transpose(pa[:, t * P:(t + 1) * P], h2[:, t, :], idf[:])
                    last.then_inc(s["h2T"], 1)
                elif n == 29:
                    pe.wait_ge(s["h2T_lo"], c + 1)
                    for t in range(NT):
                        q = slice(t * P, (t + 1) * P)
                        last = split((pb, pc)[t // 2][:, t % 2 * E:(t % 2 + 1) * E],
                                     (hid(h2_h, c)[:, q], hid(h2_l, c)[:, q]), (wr_h[:], wr_l[:]))
                        if t % 2:
                            last.then_inc(s["lg_ps"], 1)
                    split(pa[0:INTER, :], (sg_h[:], sg_l[:]), (hid(h2_h, c), hid(h2_l, c))).then_inc(s["sh_up"], 1)
                elif n == 34:
                    pe.wait_ge(s["cn_set"], c + 1)
                    for t in range(NT):
                        nc.tensor.transpose(pb[:, t * P:(t + 1) * P], cw[:, t, 0:P], idf[:])
                        last = nc.tensor.transpose(pc[0:E - P, t * P:(t + 1) * P], cw[:, t, P:E], idf[:])
                    last.then_inc(s["cT"], 1)

            def weights(i8, k):
                return bass.ds(((i8 % BODIES if isinstance(i8, int) else i8) * BODY + k) * P, P)

            def down(c, i8, k):
                pe.wait_ge(s["lo_done"], count(c, i8, k))
                w = weights(i8, k)
                return split(acc_ps[:], (wd_h[:, w], wd_l[:, w]), (gw_h[:, k, :], gw_l[:, k, :]), start=False,
                             stop=(k == BODY - 1 and isinstance(i8, int) and i8 == BODIES - 1))

            def products(c, i8, k):
                if not is_first(c, i8, k, URING):
                    pe.wait_ge(s["silu_done"], count(c, *before(i8, k, URING)))
                w = weights(i8, k)
                chunk = c + 1 if isinstance(i8, int) and i8 == BODIES else c
                split(up_ps[k % URING][:], (wg_h[:, w], wg_l[:, w]), (hid(h2_h, chunk), hid(h2_l, chunk)))\
                    .then_inc(s["up_ready"], 1)
                if isinstance(i8, int) and i8 % BODIES == 0 and k == LAG:
                    if i8:
                        pe.wait_ge(s["acc_sb"], c + 1)
                    pe.wait_ge(s["sh_lo"], chunk + 1)
                    split(acc_ps[:], (sd_h[:], sd_l[:]), (ss_h[:], ss_l[:]), stop=False)
                if not is_first(c, i8, k, LAG):
                    last = down(c, *before(i8, k, LAG))
                    if isinstance(i8, int) and i8 == BODIES and k == LAG - 1:
                        last.then_inc(s["acc_ready"], 1)

            def prologue():
                for n in range(SLOTS):
                    setup(n)
                    stage(0, n)
                for i in range(2 * NPIECE - STAGING - 2, 2 * NPIECE - STAGING):
                    piece_wait(pe, i)
                piece_wait(pe, max(i for i in range(2 * NPIECE) if i not in PIECE_DVE))

            def end(c):
                for t in range(NT):
                    last = nc.tensor.transpose(pa[:, t * P:(t + 1) * P], accs[:, t * P:(t + 1) * P], idf[:])
                last.then_inc(s["accT"], 1)

            def finish(c):
                for k in range(BODY - LAG, BODY):
                    last = down(c, BODIES - 1, k)
                last.then_inc(s["acc_ready"], 1)
                pe.wait_ge(s["acc_sb"], c + 1)
                end(c)

            chunks(pe, prologue, products, stage, end, finish)


_W = "L0_attn_"
_F = "L0_ffn_"


def kernel(**inputs):
    import numpy as np
    import concourse.bacc as bacc
    from concourse.bass_utils import run_bass_kernel_spmd

    a = {k: np.asarray(t) for k, t in inputs.items()}

    def blocks(t):
        return np.concatenate(np.split(t.reshape(t.shape[0], -1), t.shape[0] // P), 1)

    w = {k[len(_W):]: t for k, t in a.items() if k.startswith(_W)}
    f = {k[len(_F):]: t for k, t in a.items() if k.startswith(_F)}
    vecs = np.concatenate([blocks(t) for t in (
        w["norm_w"], w["in_b"], w["dwa_b"], w["sym_b"], w["pw_b"], w["fuse_b"], w["ha_b"], w["hb_b"],
        w["dwa_k"], w["sym_k"], w["A"], w["Bm"].T, a["L0_c"].T)], 1)
    mats = np.concatenate([blocks(t) for t in (
        a["L0_wmod"], w["in_w"].T, w["in_w"][DI:], w["ha_w"].T, w["hb_w"].T, w["pw_w"], w["fuse_w"].T, w["out_w"].T,
        f["router_w"].T, f["w_gate_shared"].T)], 1)
    rows = np.concatenate([f["expert_bias"], w["out_b"]])[None]
    wg = f["w_gate"].reshape(GROUPS, 2, 4, INTER, D).transpose(4, 0, 2, 3, 1).reshape(D, BLOCKS * P)
    wd = f["w_down"].reshape(GROUPS, 2, 4, D, INTER).transpose(4, 1, 0, 2, 3).reshape(P, BLOCKS * D)
    arrays = {"x": w["x"], "vecs": vecs, "mats": mats, "sdT": f["w_down_shared"].T, "rows": rows,
              "idf": np.eye(P, dtype=np.float32), "wg": wg, "wd": wd}
    arrays = {f"{k}_dram": np.ascontiguousarray(t) for k, t in arrays.items()}
    nc = bacc.Bacc("TRN2", target_bir_lowering=False, num_devices=1)
    args = [nc.dram_tensor(k, t.shape, mybir.dt.from_np(t.dtype), kind="ExternalInput").ap()
            for k, t in arrays.items()]
    out = nc.dram_tensor("out_dram", (B, L, D), F32, kind="ExternalOutput").ap()
    build(nc, *args, out)
    r = run_bass_kernel_spmd(nc, [arrays], core_ids=[0])
    return r.results[0]["out_dram"]
```
